# Optimizing a Trainium2 kernel written in Bass

```python
import numpy as np
import jax
import jax.numpy as jnp

def _softmax(x, axis=-1):
    return jax.nn.softmax(x, axis=axis)

def _gelu(x):
    return jax.nn.gelu(x, approximate=True)

def _silu(x):
    return jax.nn.silu(x)

def _sigmoid(x):
    return jax.nn.sigmoid(x)

def _layernorm(x, axis=-1, eps=1e-05):
    m = jnp.mean(x, axis=axis, keepdims=True)
    v = jnp.var(x, axis=axis, keepdims=True)
    return (x - m) / jnp.sqrt(v + eps)

def _scatter_add(tgt, idx, src, axis=0):
    return tgt.at[idx].add(src)

def _segment_sum(src, seg, n):
    return jax.ops.segment_sum(src, seg, n)
kernel_name = 'mk_seq_postln_d1_jaxref_r4_d74a36'

def setup_inputs(seed: int=0):
    np.random.seed(seed)
    _w = jnp.asarray

    def _L0_attn_setup():
        import jax, jax.numpy as jnp
        import numpy as np
        N_EMBD = 256
        BLOCK_SIZE = 512
        B = 8
        LN_EPS = 1e-05

        def _mlp(x, W1, b1, W2, b2):
            h = jax.nn.gelu(x @ W1 + b1, approximate=False)
            return h @ W2 + b2
        key = jax.random.key(seed)
        ks = jax.random.split(key, 14)
        C = N_EMBD
        std = 0.02
        d = {'x': jax.random.normal(ks[0], (B, BLOCK_SIZE, C), dtype=jnp.float32)}
        names = ['q', 'k', 'v']
        i = 1
        for n in names:
            d[f'W1{n}'] = jax.random.normal(ks[i], (C, C), dtype=jnp.float32) * std
            i += 1
            d[f'b1{n}'] = jnp.zeros((C,), dtype=jnp.float32)
            d[f'W2{n}'] = jax.random.normal(ks[i], (C, C), dtype=jnp.float32) * std
            i += 1
            d[f'b2{n}'] = jnp.zeros((C,), dtype=jnp.float32)
        d['ln_w'] = jnp.ones((C,), dtype=jnp.float32)
        d['ln_b'] = jnp.zeros((C,), dtype=jnp.float32)
        return d
    _L0_attn_in = _L0_attn_setup()

    def _L0_ffn_setup():
        import jax, jax.numpy as jnp
        import numpy as np
        LN_EPS = 1e-05
        NORM_EPS = 1e-12

        def _layernorm(x, gamma, beta):
            mu = x.mean(axis=-1, keepdims=True)
            var = ((x - mu) ** 2).mean(axis=-1, keepdims=True)
            return (x - mu) * jax.lax.rsqrt(var + LN_EPS) * gamma + beta

        def _l2norm(x, axis):
            n = jnp.sqrt((x ** 2).sum(axis=axis, keepdims=True))
            return x / jnp.maximum(n, NORM_EPS)
        key = jax.random.key(seed)
        ks = jax.random.split(key, 4)
        B, N, D, E, S, H = (64, 64, 256, 16, 16, 64)
        x = jax.random.normal(ks[0], (B, N, D), dtype=jnp.float32)
        mu = jax.random.normal(ks[1], (D, E, S), dtype=jnp.float32) / np.sqrt(D)
        w1 = jax.random.normal(ks[2], (E, D, H), dtype=jnp.float32) * np.sqrt(2.0 / D)
        w2 = jax.random.normal(ks[3], (E, H, D), dtype=jnp.float32) * np.sqrt(2.0 / (H + D))
        return {'x': x, 'ln_gamma': jnp.ones((D,), jnp.float32), 'ln_beta': jnp.zeros((D,), jnp.float32), 'mu': mu, 'scale': jnp.ones((1,), jnp.float32), 'w1': w1, 'b1': jnp.zeros((E, H), jnp.float32), 'w2': w2, 'b2': jnp.zeros((E, D), jnp.float32)}
    _L0_ffn_in = _L0_ffn_setup()
    _d = {'L0_attn_x': _L0_attn_in['x'], 'L0_attn_W1q': _L0_attn_in['W1q'], 'L0_attn_b1q': _L0_attn_in['b1q'], 'L0_attn_W2q': _L0_attn_in['W2q'], 'L0_attn_b2q': _L0_attn_in['b2q'], 'L0_attn_W1k': _L0_attn_in['W1k'], 'L0_attn_b1k': _L0_attn_in['b1k'], 'L0_attn_W2k': _L0_attn_in['W2k'], 'L0_attn_b2k': _L0_attn_in['b2k'], 'L0_attn_W1v': _L0_attn_in['W1v'], 'L0_attn_b1v': _L0_attn_in['b1v'], 'L0_attn_W2v': _L0_attn_in['W2v'], 'L0_attn_b2v': _L0_attn_in['b2v'], 'L0_attn_ln_w': _L0_attn_in['ln_w'], 'L0_attn_ln_b': _L0_attn_in['ln_b'], 'L0_ffn_ln_gamma': _L0_ffn_in['ln_gamma'], 'L0_ffn_ln_beta': _L0_ffn_in['ln_beta'], 'L0_ffn_mu': _L0_ffn_in['mu'], 'L0_ffn_scale': _L0_ffn_in['scale'], 'L0_ffn_w1': _L0_ffn_in['w1'], 'L0_ffn_b1': _L0_ffn_in['b1'], 'L0_ffn_w2': _L0_ffn_in['w2'], 'L0_ffn_b2': _L0_ffn_in['b2']}
    _x0 = _d['L0_attn_x']
    _d['L0_attn_x'] = jax.random.normal(jax.random.fold_in(jax.random.key(seed), 1), (4, 2048, 256), dtype=_x0.dtype)
    del _x0
    return _d

def reference(L0_attn_x, L0_attn_W1q, L0_attn_b1q, L0_attn_W2q, L0_attn_b2q, L0_attn_W1k, L0_attn_b1k, L0_attn_W2k, L0_attn_b2k, L0_attn_W1v, L0_attn_b1v, L0_attn_W2v, L0_attn_b2v, L0_attn_ln_w, L0_attn_ln_b, L0_ffn_ln_gamma, L0_ffn_ln_beta, L0_ffn_mu, L0_ffn_scale, L0_ffn_w1, L0_ffn_b1, L0_ffn_w2, L0_ffn_b2):

    def _L0_attn_ref(x, W1q, b1q, W2q, b2q, W1k, b1k, W2k, b2k, W1v, b1v, W2v, b2v, ln_w, ln_b):
        import jax, jax.numpy as jnp
        import numpy as np
        N_EMBD = 256
        BLOCK_SIZE = 512
        B = 8
        LN_EPS = 1e-05

        def _mlp(x, W1, b1, W2, b2):
            h = jax.nn.gelu(x @ W1 + b1, approximate=False)
            return h @ W2 + b2
        Bsz, T, C = x.shape
        q = _mlp(x, W1q, b1q, W2q, b2q)
        k = _mlp(x, W1k, b1k, W2k, b2k)
        v = _mlp(x, W1v, b1v, W2v, b2v)
        scale = np.sqrt(N_EMBD * BLOCK_SIZE).astype(np.float32)
        scores = jnp.einsum('bid,bjd->bij', q, k) / scale
        mask = jnp.tril(jnp.ones((T, T), dtype=scores.dtype))
        scores = scores * mask
        out = jnp.einsum('bij,bjd->bid', scores, v)
        mu = jnp.mean(out, axis=-1, keepdims=True)
        var = jnp.mean(jnp.square(out - mu), axis=-1, keepdims=True)
        out = (out - mu) * jax.lax.rsqrt(var + LN_EPS) * ln_w + ln_b
        return out

    def _L0_ffn_ref(x, ln_gamma, ln_beta, mu, scale, w1, b1, w2, b2):
        import jax, jax.numpy as jnp
        import numpy as np
        LN_EPS = 1e-05
        NORM_EPS = 1e-12

        def _layernorm(x, gamma, beta):
            mu = x.mean(axis=-1, keepdims=True)
            var = ((x - mu) ** 2).mean(axis=-1, keepdims=True)
            return (x - mu) * jax.lax.rsqrt(var + LN_EPS) * gamma + beta

        def _l2norm(x, axis):
            n = jnp.sqrt((x ** 2).sum(axis=axis, keepdims=True))
            return x / jnp.maximum(n, NORM_EPS)
        B, N, D = x.shape
        _, E, S = mu.shape
        xn = _layernorm(x, ln_gamma, ln_beta)
        x_unit = _l2norm(xn, axis=-1)
        mu_unit = _l2norm(mu, axis=0)
        logits = jnp.einsum('bnd,des->bnes', x_unit * scale, mu_unit)
        dispatch = jax.nn.softmax(logits, axis=1)
        combine = jax.nn.softmax(logits.reshape(B, N, E * S), axis=-1).reshape(B, N, E, S)
        slot_in = jnp.einsum('bnd,bnes->besd', xn, dispatch)
        h = jax.nn.gelu(jnp.einsum('besd,edh->besh', slot_in, w1) + b1[None, :, None, :], approximate=False)
        slot_out = jnp.einsum('besh,ehd->besd', h, w2) + b2[None, :, None, :]
        out = jnp.einsum('besd,bnes->bnd', slot_out, combine)
        return out
    x = L0_attn_x
    x = _layernorm(x + _L0_attn_ref(x, L0_attn_W1q, L0_attn_b1q, L0_attn_W2q, L0_attn_b2q, L0_attn_W1k, L0_attn_b1k, L0_attn_W2k, L0_attn_b2k, L0_attn_W1v, L0_attn_b1v, L0_attn_W2v, L0_attn_b2v, L0_attn_ln_w, L0_attn_ln_b), axis=-1)
    x = _layernorm(x + _L0_ffn_ref(x, L0_ffn_ln_gamma, L0_ffn_ln_beta, L0_ffn_mu, L0_ffn_scale, L0_ffn_w1, L0_ffn_b1, L0_ffn_w2, L0_ffn_b2), axis=-1)
    return x

_drawn_inputs = setup_inputs


def setup_inputs(seed=0):
    import zlib

    import numpy as np

    out = dict(_drawn_inputs(seed))
    spreads = {'L0_attn_b1q': (0.0, 0.1),
     'L0_attn_b2q': (0.0, 0.1),
     'L0_attn_b1k': (0.0, 0.1),
     'L0_attn_b2k': (0.0, 0.1),
     'L0_attn_b1v': (0.0, 0.1),
     'L0_attn_b2v': (0.0, 0.1),
     'L0_attn_ln_w': (1.0, 0.2),
     'L0_attn_ln_b': (0.0, 0.1),
     'L0_ffn_ln_gamma': (1.0, 0.6),
     'L0_ffn_ln_beta': (0.0, 0.7),
     'L0_ffn_b1': (0.0, 0.8),
     'L0_ffn_b2': (0.0, 0.318)}
    factors = {'L0_ffn_mu': 8.0, 'L0_ffn_w1': 3.703, 'L0_ffn_w2': 3.173}
    for name, (base, spread) in spreads.items():
        noise = np.random.default_rng([zlib.crc32(name.encode()), seed]).standard_normal(out[name].shape)
        drawn = base * np.exp(spread * noise) if base else spread * noise
        out[name] = jnp.asarray(drawn.astype(out[name].dtype))
    for name, factor in factors.items():
        out[name] = (out[name] * factor).astype(out[name].dtype)
    return out
```

```python
from contextlib import ExitStack

import concourse.bass as bass
from concourse import mybir

F32 = mybir.dt.float32
F32R = mybir.dt.float32r
ALU = mybir.AluOpType
ACT = mybir.ActivationFunctionType

P = 128
GT = 4
LN_EPS = 1e-5
NORM_EPS = 1e-12
BANK = 512


def build(nc, x, W1q, b1q, W2q, b2q, W1k, b1k, W2k, b2k, W1v, b1v, W2v, b2v, ln_w, ln_b,
          gamma, beta, mu, scale, w1, b1, w2, b2, out):
    B, T, D = x.shape
    _, E, S = mu.shape
    H = w1.shape[2]
    ES = E * S
    KB = D // P
    SB = ES // P
    TILES = B * T // P
    GROUPS = TILES // GT
    GB = GROUPS // B
    TB = TILES // B
    GTOK = GT * P
    assert D == 256 and ES == 256 and GTOK == BANK and KB == 2 and SB == 2 and H == 64
    SCORE_DIV2 = 256.0 * 512.0

    x_t = x.rearrange("b (t p) d -> p (b t) d", p=P)
    out_t = out.rearrange("b (t p) d -> p (b t) d", p=P)

    top = ExitStack()
    with top:
        def sb(name, shape, dt=F32, ctx=top):
            return ctx.enter_context(nc.sbuf_tensor(name, shape, dt))

        def sem(name, ctx=top):
            return ctx.enter_context(nc.semaphore(name))

        bank = [top.enter_context(nc.psum_tensor(f"bank{i}", [P, BANK], F32)) for i in range(8)]

        x1_all = sb("x1_all", [P, TILES, D])
        r2_all = sb("r2_all", [P, TILES])
        ident = sb("ident", [P, P])
        g_rows = sb("g_rows", [P, D])
        b_rows = sb("b_rows", [P, D])
        mu_in = sb("mu_in", [P, KB, ES])
        mu_unit = sb("mu_unit", [P, KB, ES])
        scale_col = sb("scale_col", [P, 1])
        shift = sb("shift", [P, 1])
        w1_sb = sb("w1_sb", [P, KB, E, H])
        b1T = sb("b1T", [P, E])
        b2T = sb("b2T", [P, KB, E])

        with ExitStack() as attn:
            def asb(name, shape, dt=F32):
                return sb(name, shape, dt, attn)

            def asem(name):
                return sem(name, attn)

            w_in = asb("w_in", [P, 6, KB, D])
            w_hi = asb("w_hi", [P, 6, KB, D], F32R)
            w_lo = asb("w_lo", [P, 6, KB, D], F32R)
            bias_rows = asb("bias_rows", [5 * KB, P])
            bias_col = asb("bias_col", [P, 5 * KB])
            b2v_rows = asb("b2v_rows", [P, D])
            lnw_rows = asb("lnw_rows", [P, D])
            lnb_rows = asb("lnb_rows", [P, D])
            causal = asb("causal", [P, GT, P])
            keep = asb("keep", [P, GROUPS])
            zeros = asb("zeros", [P, BANK])
            x_in = asb("x_in", [P, GT, D])
            xT_hi = asb("xT_hi", [P, KB, GTOK], F32R)
            xT_lo = asb("xT_lo", [P, KB, GTOK], F32R)
            h = asb("h", [P, 3, KB, GTOK])
            h_hi = asb("h_hi", [P, 3, KB, GTOK], F32R)
            h_lo = asb("h_lo", [P, 3, KB, GTOK], F32R)
            qT = asb("qT", [P, KB, GTOK])
            kT = asb("kT", [P, KB, GTOK])
            v_tok = asb("v_tok", [P, GT, D])
            k_tok = asb("k_tok", [P, GT, D])
            masked = asb("masked", [P, GT, P])
            state = asb("state", [P, KB, D])
            att = asb("att", [P, GT, D])
            st_o = asb("st_o", [P, GT, 6])
            mv_o = asb("mv_o", [P, GT, 2])
            rs_o = asb("rs_o", [P, GT])
            st_z = asb("st_z", [P, GT, 6])
            mv_z = asb("mv_z", [P, GT, 2])
            ve_o = asb("ve_o", [P, GT])
            ve_z = asb("ve_z", [P, 2, GT])
            r_z = asb("r_z", [P, 2, GT])
            vinv = asb("vinv", [P, GT])
            var_x1 = asb("var_x1", [P, GT])
            minus_half = asb("minus_half", [P, 2, GT])

            mu_sq = asb("mu_sq", [P, KB, ES])
            mu_inv = asb("mu_inv", [P, ES])
            ones = asb("ones", [P, P])
            mu_half = asb("mu_half", [P, ES])
            b1_row = asb("b1_row", [E, P])
            b2_row = asb("b2_row", [E, D])

            moe_loaded = asem("moe_loaded")
            b1_blank = asem("b1_blank")
            mu_squared = asem("mu_squared")
            mu_summed = asem("mu_summed")
            mu_floored = asem("mu_floored")
            mu_rs = asem("mu_rs")
            mu_scaled = asem("mu_scaled")
            mu_ready = asem("mu_ready")
            scale_neg = asem("scale_neg")
            shift_ready = asem("shift_ready")
            moe_turned = asem("moe_turned")
            moe_ready = asem("moe_ready")
            x_loaded = asem("x_loaded")
            weight_loaded = [asem(f"weight_loaded{n}") for n in range(6)]
            rows_loaded = asem("rows_loaded")
            ident_blank = asem("ident_blank")
            masks_ready = asem("masks_ready")
            keep_blank = asem("keep_blank")
            keep_ready = asem("keep_ready")
            w_rounded = asem("w_rounded")
            w_split = asem("w_split")
            bias_turned = asem("bias_turned")
            bias_ready = asem("bias_ready")
            xT_done = asem("xT_done")
            x_rounded = asem("x_rounded")
            x_split = asem("x_split")
            hidden_done = asem("hidden_done")
            h_rounded = asem("h_rounded")
            h_split = asem("h_split")
            qk_done = asem("qk_done")
            qk_ready = asem("qk_ready")
            v_done = asem("v_done")
            v_ready = asem("v_ready")
            kt_done = asem("kt_done")
            ktok_ready = asem("ktok_ready")
            scores_done = asem("scores_done")
            scores_masked = asem("scores_masked")
            state_updated = asem("state_updated")
            state_gated = asem("state_gated")
            state_copied = asem("state_copied")
            chunk_done = asem("chunk_done")
            chunk_mv = asem("chunk_mv")
            chunk_ve = asem("chunk_ve")
            chunk_rs = asem("chunk_rs")
            chunk_normed = asem("chunk_normed")
            xb_ready = asem("xb_ready")
            att_weighted = asem("att_weighted")
            z_ready = asem("z_ready")
            z_mv = asem("z_mv")
            z_ve = asem("z_ve")
            z_vinv = asem("z_vinv")
            x1_var = asem("x1_var")
            x1_ve = asem("x1_ve")
            z_rs = asem("z_rs")
            x1_ready = asem("x1_ready")
            r2_ready = asem("r2_ready")

            XT0, XT1, Q1, K1, V1, Q2, K2, V2, KT = 0, 1, 2, 4, 6, 8, 10, 12, 14
            scores_ps, state_ps, chunk_ps = bank[4], bank[5], [bank[6], bank[7]]
            LAYERS = {"q": 0, "k": 1, "v": 2}

            def job_bank(job):
                return bank[job % 4]

            def run_groups(body, engine):
                body(0, attend=False)
                with engine.Fori(1, GROUPS) as g:
                    body(g, attend=True)
                body(GROUPS, attend=True, project=False)

            block = attn.enter_context(nc.Block())

            @block.sync
            def _(sp):
                def load_x(g):
                    sp.dma_start(x_in[:, :, :], x_t[:, bass.ds(g * GT, GT), :]).then_inc(x_loaded, 16)

                load_x(0)
                for n, w in enumerate((W1q, W1k, W1v, W2q, W2k, W2v)):
                    sp.dma_start(w_in[:, n, :, :], w.rearrange("(k p) n -> p k n", p=P)).then_inc(weight_loaded[n], 16)
                for src, tile in ((gamma, g_rows), (beta, b_rows), (scale, scale_col)):
                    sp.dma_start(tile[:, :], src.partition_broadcast(P)).then_inc(moe_loaded, 16)
                sp.dma_start(mu_in[:, :, :], mu.rearrange("(k p) e s -> p k (e s)", p=P)).then_inc(moe_loaded, 16)
                sp.dma_start(b2_row[:, :], b2).then_inc(moe_loaded, 16)
                sp.wait_ge(b1_blank, 1)
                sp.dma_start(b1_row[:, 0:H], b1).then_inc(moe_loaded, 16)
                for kb in range(KB):
                    sp.dma_start(w1_sb[:, kb, :, :], w1[:, kb * P:(kb + 1) * P, :].rearrange("e p h -> p e h")
                                 ).then_inc(moe_loaded, 16)
                with sp.Fori(1, GROUPS) as g:
                    sp.wait_ge(xT_done, 2 * g)
                    sp.wait_ge(xb_ready, g)
                    load_x(g)

            @block.gpsimd
            def _(pool):
                pool.memset(ident[:, :], 0.0)
                pool.memset(causal[:, :, :], 1.0)
                pool.memset(keep[:, :], 1.0)
                pool.memset(minus_half[:, :, :], -0.5)
                pool.memset(mu_half[:, :], -0.5)
                pool.memset(ones[:, :], 1.0)
                pool.memset(b1_row[:, :], 0.0).then_inc(b1_blank, 1)
                pool.memset(zeros[:, :], 0.0).then_inc(ident_blank, 1)
                pool.wait_ge(ident_blank, 1)
                pool.affine_select(out=ident[:, :], in_=ident[:, :], compare_op=ALU.not_equal, fill=1.0,
                                   base=0, pattern=[[-1, P]], channel_multiplier=1)
                pool.affine_select(out=causal[:, :, :], in_=causal[:, :, :], compare_op=ALU.is_ge, fill=0.0,
                                   base=0, pattern=[[0, GT], [1, P]], channel_multiplier=-1)
                pool.memset(keep[:, :].rearrange("p (b g) -> p b g", g=GB)[:, :, 0:1], 0.0).then_inc(masks_ready, 1)

                def body(g, attend, project=True):
                    if project:
                        pool.wait_ge(x_loaded, 16 * (g + 1))
                        if isinstance(g, int) and g == 0:
                            pool.wait_ge(rows_loaded, 16 * 8)
                        pool.tensor_tensor(x1_all[:, bass.ds(g * GT, GT), :], x_in[:, :, :],
                                           lnb_rows[:, :].unsqueeze(1).to_broadcast([P, GT, D]),
                                           ALU.add).then_inc(xb_ready, 1)
                    if attend:
                        a = g - 1
                        for c in range(GT):
                            n = GT * a + c
                            pool.wait_ge(chunk_ve, n + 1)
                            pool.tensor_tensor(rs_o[:, c:c + 1], ve_o[:, c:c + 1], minus_half[:, 0, 0:1],
                                               ALU.pow).then_inc(chunk_rs, 1)
                            pool.wait_ge(chunk_normed, n + 1 + 2)
                            pool.tensor_tensor(att[:, c, :], att[:, c, :], lnw_rows[:, :],
                                               ALU.mult).then_inc(att_weighted, 1)
                            pool.wait_ge(att_weighted, n + 1)
                            z = x1_all[:, bass.ds(n, 1), :]
                            pool.tensor_tensor(z, z, att[:, c:c + 1, :], ALU.add).then_inc(z_ready, 1)
                        pool.wait_ge(x1_ve, a + 1)
                        pool.tensor_tensor(r_z[:, :, :], ve_z[:, :, :], minus_half[:, :, :],
                                           ALU.pow).then_inc(z_rs, 1)

                run_groups(body, pool)
                pool.wait_ge(mu_floored, 1)
                pool.tensor_tensor(mu_inv[:, :], mu_inv[:, :], mu_half[:, :], ALU.pow).then_inc(mu_rs, 1)

            @block.scalar
            def _(act):
                rows = ((b1q, 0), (b1k, 1), (b1v, 2), (b2q, 3), (b2k, 4))
                for b_row, n in rows:
                    act.dma_start(bias_rows[KB * n:KB * n + KB, :],
                                  b_row.rearrange("(k p) -> k p", p=P)).then_inc(rows_loaded, 16)
                for b_row, tile in ((b2v, b2v_rows), (ln_w, lnw_rows), (ln_b, lnb_rows)):
                    act.dma_start(tile[:, :], b_row.partition_broadcast(P)).then_inc(rows_loaded, 16)
                act.wait_ge(bias_turned, 1)
                nc.scalar.copy(bias_col[:, :], bank[7][:, 0:5 * KB]).then_inc(bias_ready, 1)
                act.wait_ge(bias_ready, 1)

                def copy_state(a, c):
                    act.wait_ge(state_updated, GT * a + c + 1)
                    if c == 0:
                        act.wait_ge(state_gated, a + 1)
                    nc.scalar.copy(state[:, :, :], state_ps[:, :].rearrange("p (k d) -> p k d", k=KB)
                                   ).then_inc(state_copied, 1)

                def round_x(g, kb):
                    act.wait_ge(xT_done, 2 * g + kb + 1)
                    nc.scalar.copy(xT_hi[:, kb, :], job_bank(XT0 + kb)[:, :]).then_inc(x_rounded, 1)

                def hidden(g, n, m):
                    act.wait_ge(hidden_done, 6 * g + 2 * n + m + 1)
                    ps = job_bank(Q1 + 2 * n + m)
                    bias = bias_col[:, KB * n + m:KB * n + m + 1]
                    nc.scalar.activation(h[:, n, m, :], ps[:, :], ACT.Gelu, bias=bias)
                    nc.scalar.activation(h_hi[:, n, m, :], ps[:, :], ACT.Gelu, bias=bias).then_inc(h_rounded, 1)

                def project_out(g, n, m):
                    act.wait_ge(qk_done, 4 * g + 2 * n + m + 1)
                    nc.scalar.activation((qT, kT)[n][:, m, :], job_bank(Q2 + 2 * n + m)[:, :], ACT.Identity,
                                         bias=bias_col[:, KB * (3 + n) + m:KB * (3 + n) + m + 1]
                                         ).then_inc(qk_ready, 1)

                def copy_k(g, m):
                    act.wait_ge(kt_done, 2 * g + m + 1)
                    nc.scalar.copy(k_tok[:, 2 * m:2 * m + 2, :],
                                   job_bank(KT + m)[:, :].rearrange("p (t d) -> p t d", t=2)
                                   ).then_inc(ktok_ready, 1)

                def body(g, attend, project=True):
                    a = g - 1
                    if attend:
                        copy_state(a, 0)
                    if project:
                        round_x(g, 0)
                        round_x(g, 1)
                    for c in range(GT):
                        if attend and c + 1 < GT:
                            copy_state(a, c + 1)
                        if project and c < 3:
                            hidden(g, c, 0)
                            hidden(g, c, 1)
                    if project:
                        for n in range(2):
                            project_out(g, n, 0)
                            project_out(g, n, 1)
                        copy_k(g, 0)
                        copy_k(g, 1)

                run_groups(body, act)
                act.wait_ge(moe_loaded, 16 * 8)
                nc.scalar.activation(mu_sq[:, :, :], mu_in[:, :, :], ACT.Square).then_inc(mu_squared, 1)
                act.wait_ge(moe_turned, 1)
                nc.scalar.copy(b1T[:, :], bank[0][:, 0:E]).then_inc(moe_ready, 1)
                nc.scalar.copy(b2T[:, :, :], bank[0][:, E:3 * E].rearrange("p (k e) -> p k e", k=KB)
                               ).then_inc(moe_ready, 1)
                act.wait_ge(moe_ready, 2)

            @block.tensor
            def _(pe):
                def split3(ps, w, xs, start, stop):
                    nc.tensor.matmul(ps, w[0], xs[0], start=start, stop=False)
                    nc.tensor.matmul(ps, w[0], xs[1], start=False, stop=False)
                    return nc.tensor.matmul(ps, w[1], xs[0], start=False, stop=stop)

                def turn_x(g, kb):
                    if kb == 0:
                        pe.wait_ge(x_loaded, 16 * (g + 1))
                    if not (isinstance(g, int) and g == 0):
                        pe.wait_ge(v_ready, 2 * g - 1 + kb)
                    for t in range(GT):
                        last = nc.tensor.transpose(job_bank(XT0 + kb)[:, t * P:(t + 1) * P],
                                                   x_in[:, t, kb * P:(kb + 1) * P], ident[:, :])
                    last.then_inc(xT_done, 1)

                def hidden(g, n, m):
                    if n == 0:
                        if m == 0:
                            pe.wait_ge(x_split, 2 * g + 2)
                        if not (isinstance(g, int) and g == 0):
                            pe.wait_ge(ktok_ready, 2 * g - 1 + m)
                    if n == 2:
                        pe.wait_ge(h_rounded, 6 * g + m + 1)
                    if isinstance(g, int) and g == 0:
                        pe.wait_ge(w_split, n + 1)
                    for kb in range(KB):
                        cols = slice(m * P, (m + 1) * P)
                        last = split3(job_bank(Q1 + 2 * n + m)[:, :],
                                      (w_hi[:, n, kb, cols], w_lo[:, n, kb, cols]),
                                      (xT_hi[:, kb, :], xT_lo[:, kb, :]), kb == 0, kb == KB - 1)
                    last.then_inc(hidden_done, 1)

                def project_qk(g, n, m):
                    pe.wait_ge(h_split, 6 * g + 2 * n + 2)
                    pe.wait_ge(h_rounded, 6 * g + 2 * (n + 1) + m + 1)
                    if isinstance(g, int) and g == 0:
                        pe.wait_ge(w_split, 3 + n + 1)
                    for kb in range(KB):
                        cols = slice(m * P, (m + 1) * P)
                        last = split3(job_bank(Q2 + 2 * n + m)[:, :],
                                      (w_hi[:, 3 + n, kb, cols], w_lo[:, 3 + n, kb, cols]),
                                      (h_hi[:, n, kb, :], h_lo[:, n, kb, :]), kb == 0, kb == KB - 1)
                    last.then_inc(qk_done, 1)

                def project_v(g, m):
                    pe.wait_ge(h_split, 6 * g + 6)
                    pe.wait_ge(qk_ready, 4 * g + m + 1)
                    if isinstance(g, int) and g == 0:
                        pe.wait_ge(w_split, 6)
                    for half in range(2):
                        toks = slice((2 * m + half) * P, (2 * m + half + 1) * P)
                        for kb in range(KB):
                            last = split3(job_bank(V2 + m)[:, half * D:(half + 1) * D],
                                          (h_hi[:, 2, kb, toks], h_lo[:, 2, kb, toks]),
                                          (w_hi[:, 5, kb, :], w_lo[:, 5, kb, :]), kb == 0, kb == KB - 1)
                    last.then_inc(v_done, 1)

                def turn_k(g, m):
                    pe.wait_ge(qk_ready, 4 * g + 4)
                    for half in range(2):
                        for kb in range(KB):
                            at = half * D + kb * P
                            last = nc.tensor.transpose(
                                job_bank(KT + m)[:, at:at + P],
                                kT[:, kb, (2 * m + half) * P:(2 * m + half + 1) * P], ident[:, :])
                    last.then_inc(kt_done, 1)

                def scores(a):
                    pe.wait_ge(scores_masked, a + 1)
                    pe.wait_ge(qk_ready, 4 * a + 4)
                    for c in range(GT):
                        toks = slice(c * P, (c + 1) * P)
                        for kb in range(KB):
                            last = nc.tensor.matmul(scores_ps[:, toks], kT[:, kb, toks], qT[:, kb, toks],
                                                    start=(kb == 0), stop=(kb == KB - 1))
                    last.then_inc(scores_done, 1)

                def chunk(a, c):
                    toks = slice(c * P, (c + 1) * P)
                    ps = chunk_ps[c % 2][:, 0:D]
                    pe.wait_ge(chunk_normed, GT * a + c + 1)
                    pe.wait_ge(state_copied, GT * a + c + 1)
                    for kb in range(KB):
                        nc.tensor.matmul(ps, qT[:, kb, toks], state[:, kb, :], start=(kb == 0), stop=False)
                    if c == 0:
                        pe.wait_ge(scores_masked, a + 2)
                        pe.wait_ge(v_ready, 2 * a + 2)
                    nc.tensor.matmul(ps, masked[:, c, :], v_tok[:, c, :], start=False,
                                     stop=True).then_inc(chunk_done, 1)
                    if c == 0:
                        pe.wait_ge(ktok_ready, 2 * a + 2)
                    for kb in range(KB):
                        last = nc.tensor.matmul(state_ps[:, kb * D:(kb + 1) * D], k_tok[:, c, kb * P:(kb + 1) * P],
                                                v_tok[:, c, :], start=False, stop=False, skip_group_check=True)
                    last.then_inc(state_updated, 1)

                def body(g, attend, project=True):
                    a = g - 1
                    if attend:
                        scores(a)
                    if project:
                        turn_x(g, 0)
                        turn_x(g, 1)
                    for c in range(GT):
                        if attend:
                            chunk(a, c)
                        if project and c < 3:
                            hidden(g, c, 0)
                            hidden(g, c, 1)
                    if project:
                        for n in range(2):
                            project_qk(g, n, 0)
                            project_qk(g, n, 1)
                        project_v(g, 0)
                        project_v(g, 1)
                        turn_k(g, 0)
                        turn_k(g, 1)

                pe.wait_ge(masks_ready, 1)
                pe.wait_ge(rows_loaded, 16 * 8)
                nc.tensor.transpose(bank[7][:, 0:5 * KB], bias_rows[:, :], ident[0:5 * KB, 0:5 * KB]
                                    ).then_inc(bias_turned, 1)
                nc.tensor.matmul(state_ps[:, :], ident[:, :], zeros[:, :], start=True, stop=True
                                 ).then_inc(state_updated, 1)
                pe.wait_ge(bias_ready, 1)
                run_groups(body, pe)
                pe.wait_ge(moe_loaded, 16 * 8)
                pe.wait_ge(mu_squared, 1)
                nc.tensor.transpose(bank[0][:, 0:E], b1_row[:, :], ident[0:E, 0:E])
                for kb in range(KB):
                    last = nc.tensor.transpose(bank[0][:, (1 + kb) * E:(2 + kb) * E],
                                               b2_row[:, kb * P:(kb + 1) * P], ident[0:E, 0:E])
                last.then_inc(moe_turned, 1)
                for kb in range(KB):
                    last = nc.tensor.matmul(bank[1][:, 0:ES], ones[:, :], mu_sq[:, kb, :], start=(kb == 0),
                                            stop=(kb == KB - 1))
                last.then_inc(mu_summed, 1)

            @block.vector
            def _(dve):
                nc.vector.memset(rs_o[:, :], 0.0).then_inc(chunk_normed, 2)
                nc.vector.memset(var_x1[:, :], 0.0).then_inc(scores_masked, 1)
                nc.vector.memset(vinv[:, :], 0.0).then_inc(z_ready, 1)
                for n in range(6):
                    dve.wait_ge(weight_loaded[n], 16)
                    nc.vector.tensor_copy(w_hi[:, n, :, :], w_in[:, n, :, :]).then_inc(w_rounded, 1)
                    dve.wait_ge(w_rounded, n + 1)
                    nc.vector.tensor_tensor(w_lo[:, n, :, :], w_in[:, n, :, :], w_hi[:, n, :, :].bitcast(F32),
                                            ALU.subtract).then_inc(w_split, 1)
                dve.wait_ge(masks_ready, 1)

                def gate_state(a):
                    dve.wait_ge(state_updated, GT * a + 1)
                    nc.vector.tensor_scalar(state_ps[:, :], state_ps[:, :], keep[:, bass.ds(a, 1)], None,
                                            ALU.mult).then_inc(state_gated, 1)

                def mask_scores(a):
                    dve.wait_ge(scores_done, a + 1)
                    nc.vector.tensor_tensor(masked[:, :, :], scores_ps[:, :].rearrange("p (c n) -> p c n", c=GT),
                                            causal[:, :, :], ALU.mult).then_inc(scores_masked, 1)

                def split_x(g, kb):
                    dve.wait_ge(x_rounded, 2 * g + kb + 1)
                    nc.vector.tensor_tensor(xT_lo[:, kb, :], job_bank(XT0 + kb)[:, :],
                                            xT_hi[:, kb, :].bitcast(F32), ALU.subtract).then_inc(x_split, 1)

                def split_h(g, n, m):
                    dve.wait_ge(h_rounded, 6 * g + 2 * n + m + 1)
                    nc.vector.tensor_tensor(h_lo[:, n, m, :], h[:, n, m, :], h_hi[:, n, m, :].bitcast(F32),
                                            ALU.subtract).then_inc(h_split, 1)

                def bias_v(g, m):
                    dve.wait_ge(v_done, 2 * g + m + 1)
                    nc.vector.tensor_tensor(v_tok[:, 2 * m:2 * m + 2, :],
                                            job_bank(V2 + m)[:, :].rearrange("p (t d) -> p t d", t=2),
                                            b2v_rows[:, :].unsqueeze(1).to_broadcast([P, 2, D]),
                                            ALU.add).then_inc(v_ready, 1)

                def chunk_statistics(a, c):
                    n = GT * a + c
                    dve.wait_ge(chunk_done, n + 1)
                    nc.vector.bn_stats(st_o[:, c, :], chunk_ps[c % 2][:, 0:D])
                    dve.drain()
                    nc.vector.bn_aggr(mv_o[:, c, :], st_o[:, c, :]).then_inc(chunk_mv, 1)
                    dve.wait_ge(chunk_mv, n + 1)
                    nc.vector.tensor_scalar(ve_o[:, c:c + 1], mv_o[:, c, 1:2], LN_EPS * SCORE_DIV2, None,
                                            ALU.add).then_inc(chunk_ve, 1)

                def norm_chunk(a, c):
                    n = GT * a + c
                    dve.wait_ge(chunk_rs, n + 1)
                    if c == 0:
                        dve.wait_ge(z_ready, GT * a + 1)
                    nc.vector.tensor_scalar(att[:, c, :], chunk_ps[c % 2][:, 0:D], mv_o[:, c, 0:1],
                                            rs_o[:, c:c + 1], ALU.subtract, ALU.mult).then_inc(chunk_normed, 1)

                def z_statistics(a, c):
                    n = GT * a + c
                    dve.wait_ge(z_ready, n + 2)
                    nc.vector.bn_stats(st_z[:, c, :], x1_all[:, bass.ds(n, 1), :])
                    dve.drain()
                    nc.vector.bn_aggr(mv_z[:, c, :], st_z[:, c, :]).then_inc(z_mv, 1)

                def norm_z(a):
                    var = mv_z[:, :, 1]
                    dve.wait_ge(z_mv, GT * a + GT)
                    nc.vector.tensor_scalar(ve_z[:, 0, :], var, LN_EPS, None, ALU.add).then_inc(z_ve, 1)
                    dve.wait_ge(z_ve, a + 1)
                    nc.vector.reciprocal(vinv[:, :], ve_z[:, 0, :]).then_inc(z_vinv, 1)
                    dve.wait_ge(z_vinv, a + 1)
                    nc.vector.tensor_tensor(var_x1[:, :], var, vinv[:, :], ALU.mult).then_inc(x1_var, 1)
                    dve.wait_ge(x1_var, a + 1)
                    nc.vector.tensor_scalar(ve_z[:, 1, :], var_x1[:, :], LN_EPS, None, ALU.add).then_inc(x1_ve, 1)
                    dve.wait_ge(z_rs, a + 1)
                    for c in range(GT):
                        xc = x1_all[:, bass.ds(GT * a + c, 1), :]
                        nc.vector.tensor_scalar(xc, xc, mv_z[:, c, 0:1], r_z[:, 0, c:c + 1],
                                                ALU.subtract, ALU.mult).then_inc(x1_ready, 1)
                    nc.vector.tensor_copy(r2_all[:, bass.ds(GT * a, GT)], r_z[:, 1, :]).then_inc(r2_ready, 1)

                def body(g, attend, project=True):
                    a = g - 1
                    if attend:
                        gate_state(a)
                        mask_scores(a)
                    if project:
                        split_x(g, 0)
                        split_x(g, 1)
                    for c in range(GT):
                        if attend:
                            chunk_statistics(a, c)
                        if project and c < 3:
                            split_h(g, c, 0)
                            split_h(g, c, 1)
                        if attend:
                            norm_chunk(a, c)
                            if c > 0:
                                z_statistics(a, c - 1)
                    if attend:
                        z_statistics(a, GT - 1)
                        norm_z(a)
                    if project:
                        bias_v(g, 0)
                        bias_v(g, 1)

                run_groups(body, dve)
                dve.wait_ge(moe_loaded, 16 * 8)
                nc.vector.tensor_scalar(shift[:, :], scale_col[:, :], -1.0, None, ALU.mult).then_inc(scale_neg, 1)
                dve.wait_ge(scale_neg, 1)
                nc.vector.tensor_tensor(shift[:, :], shift[:, :], scale_col[:, :], ALU.min).then_inc(shift_ready, 1)
                dve.wait_ge(mu_summed, 1)
                nc.vector.tensor_scalar(mu_inv[:, :], bank[1][:, 0:ES], NORM_EPS ** 2, None, ALU.max
                                        ).then_inc(mu_floored, 1)
                dve.wait_ge(mu_rs, 1)
                nc.vector.tensor_scalar(mu_inv[:, :], mu_inv[:, :], scale_col[:, :], None,
                                        ALU.mult).then_inc(mu_scaled, 1)
                dve.wait_ge(mu_scaled, 1)
                for kb in range(KB):
                    nc.vector.tensor_tensor(mu_unit[:, kb, :], mu_in[:, kb, :], mu_inv[:, :],
                                            ALU.mult).then_inc(mu_ready, 1)
                dve.wait_ge(shift_ready, 1)
                dve.wait_ge(mu_ready, KB)
                dve.wait_ge(x1_ready, TILES)
                dve.wait_ge(r2_ready, GROUPS)

        with ExitStack() as moe:
            def msb(name, shape, dt=F32):
                return sb(name, shape, dt, moe)

            def msem(name):
                return sem(name, moe)

            ET_all = msb("ET_all", [P, SB, TILES * P])
            rsum = msb("rsum", [P, TILES])
            rinv = msb("rinv", [P, TILES])
            xn = [msb(f"xn{q}", [P, GT, D + 1]) for q in range(GB)]
            xnT = [msb(f"xnT{q}", [P, KB, GTOK]) for q in range(2)]
            square = msb("square", [P, 2, D])
            n2 = msb("n2", [P, GB, GT])
            n2_low = msb("n2_low", [P, GB, GT])
            xinv = msb("xinv", [P, GB, GT])
            minus_half = msb("minus_half2", [P, GT])
            e_tok = msb("e_tok", [P, 4, ES])
            colinv = msb("colinv", [P, SB])
            slot_in = msb("slot_in", [P, SB, D])
            slot_inT = msb("slot_inT", [P, KB, B, ES])
            w2_sb = msb("w2_sb", [H, E, D])

            w2_loaded = msem("w2_loaded")
            half_set = msem("half_set")
            ones_set = msem("ones_set")
            tok_scaled = msem("tok_scaled")
            xn_ready = msem("xn_ready")
            n2_ready = msem("n2_ready")
            n2_floored = msem("n2_floored")
            xinv_ready = msem("xinv_ready")
            xnT_done = msem("xnT_done")
            xnT_ready = msem("xnT_ready")
            logits_done = msem("logits_done")
            e_ready = msem("e_ready")
            eT_done = msem("eT_done")
            eT_ready = msem("eT_ready")
            tile_folded = msem("tile_folded")
            rinv_ready = msem("rinv_ready")
            colinv_ready = msem("colinv_ready")
            slot_in_ready = msem("slot_in_ready")
            slot_in_turned = msem("slot_in_turned")
            slot_inT_ready = msem("slot_inT_ready")

            xnT_ps, log_ps, eT_ps, fold_ps = bank[0:2], bank[2:4], bank[4:6], bank[6:8]

            hs = e_tok[0:H, :, :].rearrange("p i (e n) -> p (i e) n", n=B * S)
            soT = slot_inT
            so = w1_sb[:, :, :, :].rearrange("p k (b e) (s h) -> p (k b) (e s h)", b=2, s=1
                                             ).rearrange("p b (s d) -> p b s d", s=SB)
            hs_done = msem("hs_done")
            hs_biased = msem("hs_biased")
            hs_ready = msem("hs_ready")
            soT_done = msem("soT_done")
            soT_ready = msem("soT_ready")
            so_done = msem("so_done")
            so_ready = msem("so_ready")

            eT = xnT
            y = xn
            st_y = msb("st_y", [P, GT, 6])
            mv_y = msb("mv_y", [P, 2, GT, 2])
            ve_y = msb("ve_y", [P, 2, GT])
            rs_y = msb("rs_y", [P, 2, GT])
            eT_staged = msem("eT_staged")
            mixed = msem("mixed")
            mix_scaled = msem("mix_scaled")
            y_ready = msem("y_ready")
            y_mv = msem("y_mv")
            y_ve = msem("y_ve")
            y_rs = msem("y_rs")
            y_normed = msem("y_normed")
            stored = [msem(f"stored{q}") for q in range(GB)]
            mix_ps = bank[0:4]

            block = moe.enter_context(nc.Block())

            @block.sync
            def _(sp):
                sp.dma_start(w2_sb[:, :, :], w2.rearrange("e h d -> h e d")).then_inc(w2_loaded, 16)
                with sp.Fori(0, B) as b:
                    for q in range(GB):
                        k = GB * b + q
                        sp.wait_ge(y_normed, GT * k + GT)
                        sp.dma_start(out_t[:, bass.ds(GT * k, GT), :], y[q][:, :, 0:D]).then_inc(stored[q], 16)
                for q in range(GB):
                    sp.wait_ge(stored[q], 16 * B + 16)

            @block.gpsimd
            def _(pool):
                pool.memset(minus_half[:, :], -0.5).then_inc(half_set, 1)
                pool.wait_ge(half_set, 1)

                def invert_norms(b, q):
                    pool.wait_ge(n2_floored, GB * b + q + 1)
                    pool.tensor_tensor(xinv[:, q, :], n2_low[:, q, :], minus_half[:, :],
                                       ALU.pow).then_inc(xinv_ready, 1)

                with pool.Fori(0, B) as b:
                    for q in range(GB):
                        pool.wait_ge(tok_scaled, GT * GB * b + GT * q + GT)
                        pool.tensor_tensor(xn[q][:, :, 0:D], xn[q][:, :, 0:D],
                                           b_rows[:, :].unsqueeze(1).to_broadcast([P, GT, D]),
                                           ALU.add).then_inc(xn_ready, 1)
                        invert_norms(b, q)

                def add_residual(k, q):
                    pool.wait_ge(mix_scaled, GT * k + GT + 4)
                    yq = y[q][:, :, 0:D]
                    pool.tensor_tensor(yq, yq, x1_all[:, bass.ds(GT * k, GT), :], ALU.add).then_inc(y_ready, 1)

                def invert_deviation(k, q):
                    pool.wait_ge(y_ve, k + 1)
                    pool.tensor_tensor(rs_y[:, q % 2, :], ve_y[:, q % 2, :], minus_half[:, :], ALU.pow).then_inc(y_rs, 1)

                def finish(b, last):
                    for q in range(GB):
                        if not (last and q == GB - 1):
                            add_residual(GB * b + q + 1, (q + 1) % GB)
                        invert_deviation(GB * b + q, q)

                add_residual(0, 0)
                with pool.Fori(0, B - 1) as b:
                    finish(b, last=False)
                finish(B - 1, last=True)

            @block.scalar
            def _(act):
                def norms(b, q):
                    act.wait_ge(xn_ready, GB * b + q + 1)
                    for t in range(GT):
                        act.wait_ge(n2_ready, GT * (GB * b + q) + max(t - 1, 0) + 1)
                        nc.scalar.activation(square[:, t % 2, :], xn[q][:, t, 0:D], ACT.Square,
                                             accum_out=n2[:, q, t:t + 1]).then_inc(n2_ready, 1)

                def copy_xnT(b, q):
                    act.wait_ge(xnT_done, GB * b + q + 1)
                    for kb in range(KB):
                        nc.scalar.copy(xnT[q % 2][:, kb, :], xnT_ps[kb][:, :]).then_inc(xnT_ready, 1)

                def exps(b, t):
                    q = t // GT
                    act.wait_ge(logits_done, TB * b + t + 1)
                    act.wait_ge(xinv_ready, GB * b + q + 1)
                    nc.scalar.activation(e_tok[:, t % 4, :], log_ps[t % 2][:, 0:ES], ACT.Exp, bias=shift[:, :],
                                         scale=xinv[:, q, t % GT:t % GT + 1],
                                         accum_out=rsum[:, bass.ds(TB * b + t, 1)]).then_inc(e_ready, 1)

                with act.Fori(0, B) as b:
                    norms(b, 0)
                    copy_xnT(b, 0)
                    for t in range(TB):
                        exps(b, t)
                        q = t // GT
                        if t % GT == 0 and q + 1 < GB:
                            norms(b, q + 1)
                        if t % GT == 1 and q + 1 < GB:
                            copy_xnT(b, q + 1)
                    act.wait_ge(slot_in_turned, b + 1)
                    for db in range(KB):
                        nc.scalar.copy(slot_inT[:, db, bass.ds(b, 1), :], xnT_ps[db][:, 0:ES].unsqueeze(1)
                                       ).then_inc(slot_inT_ready, 1)
                for half in range(2):
                    act.wait_ge(hs_biased, half + 1)
                    eh = slice(half * E // 2, (half + 1) * E // 2)
                    nc.scalar.activation(hs[:, eh, :], hs[:, eh, :], ACT.Gelu).then_inc(hs_ready, 1)
                for n in range(4):
                    act.wait_ge(so_done, n + 1)
                    nc.scalar.copy(so[:, n, :, :], bank[(6, 7, 0, 1)[n]][:, :].rearrange("p (s d) -> p s d", s=SB)
                                   ).then_inc(so_ready, 1)

                def stage_eT(k, q):
                    act.wait_ge(mixed, GT * k + GT)
                    nc.scalar.copy(eT[q % 2][:, :, :], ET_all[:, :, bass.ds(k * GTOK, GTOK)]
                                   ).then_inc(eT_staged, 1)

                def scale_mix(b, q):
                    k = GB * b + q
                    act.wait_ge(stored[q], 16 * b + 16)
                    for t in range(GT):
                        act.wait_ge(mixed, GT * k + t + 1 + 2 * GT)
                        nc.scalar.activation(y[q][:, t, 0:D], mix_ps[t][:, 0:D], ACT.Copy,
                                             scale=rinv[:, bass.ds(GT * k + t, 1)]).then_inc(mix_scaled, 1)

                def combine(b, last):
                    for q in range(GB):
                        if not (last and q == GB - 1):
                            stage_eT(GB * b + q + 1, (q + 1) % GB)
                        scale_mix(b, q)

                act.wait_ge(eT_ready, TILES + 2)
                act.wait_ge(rinv_ready, B)
                stage_eT(0, 0)
                with act.Fori(0, B - 1) as b:
                    combine(b, last=False)
                combine(B - 1, last=True)

            @block.tensor
            def _(pe):
                pe.wait_ge(ones_set, GB)

                def turn_xn(b, q):
                    pe.wait_ge(xn_ready, GB * b + q + 1)
                    if q == 0:
                        pe.wait_ge(slot_inT_ready, KB * b + KB)
                    else:
                        pe.wait_ge(xnT_ready, KB * (GB * b + q))
                    for kb in range(KB):
                        for t in range(GT):
                            last = nc.tensor.transpose(xnT_ps[kb][:, t * P:(t + 1) * P],
                                                       xn[q][:, t, kb * P:(kb + 1) * P], ident[:, :])
                    last.then_inc(xnT_done, 1)

                def logits(b, t):
                    q = t // GT
                    if t % GT == 0:
                        pe.wait_ge(xnT_ready, KB * (GB * b + q + 1))
                    pe.wait_ge(e_ready, TB * b + t + 1)
                    for kb in range(KB):
                        last = nc.tensor.matmul(log_ps[t % 2][:, 0:ES],
                                                xnT[q % 2][:, kb, (t % GT) * P:(t % GT + 1) * P],
                                                mu_unit[:, kb, :], start=(kb == 0), stop=(kb == KB - 1))
                    last.then_inc(logits_done, 1)

                def fold(b, t):
                    q = t // GT
                    pe.wait_ge(e_ready, TB * b + t + 3)
                    pe.wait_ge(eT_ready, TB * b + t + 1)
                    for s in range(SB):
                        last = nc.tensor.transpose(eT_ps[t % 2][:, s * P:(s + 1) * P],
                                                   e_tok[:, t % 4, s * P:(s + 1) * P], ident[:, :])
                    last.then_inc(eT_done, 1)
                    if t == 0:
                        pe.wait_ge(slot_in_ready, SB * b + SB)
                    for s in range(SB):
                        last = nc.tensor.matmul(fold_ps[s][:, 0:D + 1], e_tok[:, t % 4, s * P:(s + 1) * P],
                                                xn[q][:, t % GT, :], start=(t == 0), stop=(t == TB - 1))
                    last.then_inc(tile_folded, 1)

                LAG = 2
                with pe.Fori(0, B) as b:
                    turn_xn(b, 0)
                    for t in range(TB + LAG):
                        if t < TB:
                            logits(b, t)
                        if t % GT == 1 and t // GT + 1 < GB:
                            turn_xn(b, t // GT + 1)
                        if t >= LAG:
                            fold(b, t - LAG)
                    pe.wait_ge(slot_in_ready, SB * b + 2 * SB)
                    for db in range(KB):
                        for s in range(SB):
                            last = nc.tensor.transpose(xnT_ps[db][:, s * P:(s + 1) * P],
                                                       slot_in[:, s, db * P:(db + 1) * P], ident[:, :])
                    last.then_inc(slot_in_turned, 1)

                pe.wait_ge(slot_inT_ready, KB * B + KB)
                for e in range(E):
                    ps = bank[2 + e // 8][0:H, (e % 8) * B * S:(e % 8 + 1) * B * S]
                    for kb in range(KB):
                        last = nc.tensor.matmul(ps, w1_sb[:, kb, e, :], slot_inT[:, kb, :, e * S:(e + 1) * S],
                                                start=(kb == 0), stop=(kb == KB - 1))
                    if e % 8 == 7:
                        last.then_inc(hs_done, 1)
                pe.wait_ge(w2_loaded, 16)
                for half in range(2):
                    pe.wait_ge(hs_ready, half + 1)
                    for db in range(KB):
                        ps = bank[(4, 0)[db] + half]
                        for e in range(8 * half, 8 * half + 8):
                            last = nc.tensor.matmul(ps[:, (e % 8) * B * S:(e % 8 + 1) * B * S],
                                                    w2_sb[:, e, db * P:(db + 1) * P], hs[:, e, :],
                                                    start=True, stop=True)
                        last.then_inc(soT_done, 1)
                pe.wait_ge(soT_ready, 4)
                for n in range(B):
                    for s in range(SB):
                        for db in range(KB):
                            at = s * D + db * P
                            last = nc.tensor.transpose(bank[(6, 7, 0, 1)[n]][:, at:at + P],
                                                       soT[:, db, n, s * P:(s + 1) * P], ident[:, :])
                    last.then_inc(so_done, 1)
                pe.wait_ge(so_ready, 4)
                with pe.Fori(0, B) as b:
                    for q in range(GB):
                        k = GB * b + q
                        pe.wait_ge(eT_staged, k + 1)
                        for t in range(GT):
                            pe.wait_ge(mix_scaled, GT * k + t + 1)
                            for s in range(SB):
                                last = nc.tensor.matmul(mix_ps[t][:, 0:D], eT[q % 2][:, s, t * P:(t + 1) * P],
                                                        so[:, bass.ds(b, 1), s, :], start=(s == 0),
                                                        stop=(s == SB - 1))
                            last.then_inc(mixed, 1)

            @block.vector
            def _(dve):
                nc.vector.memset(st_y[:, 0, :], 0.0).then_inc(e_ready, 2)
                nc.vector.memset(st_y[:, 1, :], 0.0).then_inc(eT_ready, 2)
                nc.vector.memset(st_y[:, 2, :], 0.0).then_inc(tile_folded, TB)
                nc.vector.memset(st_y[:, 3, :], 0.0).then_inc(mixed, 2 * GT)
                nc.vector.memset(n2[:, :, :], 0.0).then_inc(slot_in_ready, SB)
                nc.vector.memset(xinv[:, :, :], 0.0).then_inc(slot_inT_ready, KB)
                nc.vector.memset(colinv[:, :], 0.0).then_inc(mix_scaled, 4)
                nc.vector.memset(mv_y[:, 0, :, :], 0.0).then_inc(n2_ready, 1)
                for q in range(GB):
                    nc.vector.memset(mv_y[:, 1, q, :], 0.0).then_inc(stored[q], 16)
                for q in range(GB):
                    nc.vector.memset(xn[q][:, :, D:D + 1], 1.0).then_inc(ones_set, 1)

                def scale_tokens(b, q):
                    k = GB * b + q
                    dve.wait_ge(tile_folded, GT * k + GT)
                    for t in range(GT):
                        tile = GT * k + t
                        nc.vector.scalar_tensor_tensor(
                            out=xn[q][:, t, 0:D], in0=x1_all[:, bass.ds(tile, 1), :].rearrange("p o d -> p (o d)"),
                            scalar=r2_all[:, bass.ds(tile, 1)], in1=g_rows[:, :],
                            op0=ALU.mult, op1=ALU.mult).then_inc(tok_scaled, 1)

                def invert_norms(b, q):
                    dve.wait_ge(n2_ready, GT * (GB * b + q) + GT + 1)
                    nc.vector.tensor_scalar(n2_low[:, q, :], n2[:, q, :], NORM_EPS ** 2, None, ALU.max
                                            ).then_inc(n2_floored, 1)

                def copy_eT(b, t):
                    dve.wait_ge(eT_done, TB * b + t + 1)
                    nc.vector.tensor_copy(ET_all[:, :, bass.ds((TB * b + t) * P, P)],
                                          eT_ps[t % 2][:, 0:ES].rearrange("p (s n) -> p s n", s=SB)
                                          ).then_inc(eT_ready, 1)

                with dve.Fori(0, B) as b:
                    scale_tokens(b, 0)
                    invert_norms(b, 0)
                    scale_tokens(b, 1)
                    for t in range(TB):
                        q = t // GT
                        if t % GT == 1 and q + 1 < GB:
                            invert_norms(b, q + 1)
                        if t % GT == 2 and q + 2 < GB:
                            scale_tokens(b, q + 2)
                        copy_eT(b, t)
                    nc.vector.reciprocal(rinv[:, bass.ds(TB * b, TB)], rsum[:, bass.ds(TB * b, TB)]
                                         ).then_inc(rinv_ready, 1)
                    dve.wait_ge(tile_folded, TB * b + 2 * TB)
                    for s in range(SB):
                        nc.vector.reciprocal(colinv[:, s:s + 1], fold_ps[s][:, D:D + 1]).then_inc(colinv_ready, 1)
                    for s in range(SB):
                        dve.wait_ge(colinv_ready, SB * b + s + 1)
                        nc.vector.tensor_scalar(slot_in[:, s, :], fold_ps[s][:, 0:D], colinv[:, s:s + 1], None,
                                                ALU.mult).then_inc(slot_in_ready, 1)

                for half in range(2):
                    dve.wait_ge(hs_done, half + 1)
                    eh = slice(half * E // 2, (half + 1) * E // 2)
                    nc.vector.tensor_tensor(hs[:, eh, :],
                                            bank[2 + half][0:H, :].rearrange("p (e n) -> p e n", e=E // 2),
                                            b1T[0:H, eh].unsqueeze(2).to_broadcast([H, E // 2, B * S]),
                                            ALU.add).then_inc(hs_biased, 1)
                for half in range(2):
                    for db in range(KB):
                        dve.wait_ge(soT_done, KB * half + db + 1)
                        eh = slice(half * E // 2, (half + 1) * E // 2)
                        for n in range(B):
                            last = nc.vector.tensor_tensor(
                                soT[:, db, n, :].rearrange("p (e s) -> p e s", s=S)[:, eh, :],
                                bank[(4, 0)[db] + half][:, :].rearrange("p (e n s) -> p e n s", n=B, s=S)[:, :, n, :],
                                b2T[:, db, eh].unsqueeze(2).to_broadcast([P, E // 2, S]), ALU.add)
                        last.then_inc(soT_ready, 1)

                def y_statistics(k, q):
                    dve.wait_ge(y_ready, k + 1)
                    for t in range(GT):
                        nc.vector.bn_stats(st_y[:, t, :], y[q][:, t, 0:D])
                    dve.drain()
                    for t in range(GT):
                        nc.vector.bn_aggr(mv_y[:, q % 2, t, :], st_y[:, t, :]).then_inc(y_mv, 1)
                    dve.wait_ge(y_mv, GT * k + GT)
                    nc.vector.tensor_scalar(ve_y[:, q % 2, :], mv_y[:, q % 2, :, 1], LN_EPS, None,
                                            ALU.add).then_inc(y_ve, 1)

                def norm_y(k, q):
                    dve.wait_ge(y_rs, k + 1)
                    for t in range(GT):
                        nc.vector.tensor_scalar(y[q][:, t, 0:D], y[q][:, t, 0:D], mv_y[:, q % 2, t, 0:1],
                                                rs_y[:, q % 2, t:t + 1], ALU.subtract, ALU.mult).then_inc(y_normed, 1)

                def finish(b, last):
                    for q in range(GB):
                        if not (last and q == GB - 1):
                            y_statistics(GB * b + q + 1, (q + 1) % GB)
                        norm_y(GB * b + q, q)

                y_statistics(0, 0)
                with dve.Fori(0, B - 1) as b:
                    finish(b, last=False)
                finish(B - 1, last=True)
        return nc


_INS = ["x", "W1q", "b1q", "W2q", "b2q", "W1k", "b1k", "W2k", "b2k", "W1v", "b1v", "W2v", "b2v", "ln_w", "ln_b",
        "ln_gamma", "ln_beta", "mu", "scale", "w1", "b1", "w2", "b2"]
_NAMES = ["L0_attn_" + n for n in _INS[:15]] + ["L0_ffn_" + n for n in _INS[15:]]


def kernel(**inputs):
    import numpy as _np
    import concourse.bacc as _bacc
    from concourse import mybir as _mybir
    from concourse.bass_utils import run_bass_kernel_spmd as _run

    nc = _bacc.Bacc("TRN2", target_bir_lowering=False, num_devices=1)
    arrays, args = {}, []
    for name in _NAMES:
        a = _np.ascontiguousarray(inputs[name])
        arrays[f"in_{name}"] = a
        args.append(nc.dram_tensor(f"in_{name}", a.shape, _mybir.dt.from_np(a.dtype), kind="ExternalInput").ap())
    shape = inputs["L0_attn_x"].shape
    args.append(nc.dram_tensor("out_0", shape, _mybir.dt.from_np(_np.dtype("float32")), kind="ExternalOutput").ap())
    build(nc, *args)
    r = _run(nc, [arrays], core_ids=[0])
    return r.results[0]["out_0"]
```

```python
from contextlib import ExitStack

import concourse.bass as bass
from concourse import mybir

F32 = mybir.dt.float32
F32R = mybir.dt.float32r
ALU = mybir.AluOpType
ACT = mybir.ActivationFunctionType

P = 128
GT = 4
LN_EPS = 1e-5
NORM_EPS = 1e-12
BANK = 512


def build(nc, x, W1q, b1q, W2q, b2q, W1k, b1k, W2k, b2k, W1v, b1v, W2v, b2v, ln_w, ln_b,
          gamma, beta, mu, scale, w1, b1, w2, b2, out):
    B, T, D = x.shape
    _, E, S = mu.shape
    H = w1.shape[2]
    ES = E * S
    KB = D // P
    SB = ES // P
    TILES = B * T // P
    GROUPS = TILES // GT
    GB = GROUPS // B
    TB = TILES // B
    GTOK = GT * P
    assert D == 256 and ES == 256 and GTOK == BANK and KB == 2 and SB == 2 and H == 64
    SCORE_DIV2 = 256.0 * 512.0

    x_t = x.rearrange("b (t p) d -> p (b t) d", p=P)
    out_t = out.rearrange("b (t p) d -> p (b t) d", p=P)

    top = ExitStack()
    with top:
        def sb(name, shape, dt=F32, ctx=top):
            return ctx.enter_context(nc.sbuf_tensor(name, shape, dt))

        def sem(name, ctx=top):
            return ctx.enter_context(nc.semaphore(name))

        bank = [top.enter_context(nc.psum_tensor(f"bank{i}", [P, BANK], F32)) for i in range(8)]

        x1_all = sb("x1_all", [P, TILES, D])
        r2_all = sb("r2_all", [P, TILES])
        ident = sb("ident", [P, P])
        g_rows = sb("g_rows", [P, D])
        b_rows = sb("b_rows", [P, D])
        mu_hi = sb("mu_hi", [P, KB, ES], F32R)
        mu_lo = sb("mu_lo", [P, KB, ES], F32R)
        scale_col = sb("scale_col", [P, 1])
        shift = sb("shift", [P, 1])
        b1T = sb("b1T", [P, E])
        b2T = sb("b2T", [P, KB, E])

        with ExitStack() as attn:
            def asb(name, shape, dt=F32):
                return sb(name, shape, dt, attn)

            def asem(name):
                return sem(name, attn)

            scratch = asb("scratch", [P, 3, KB * GTOK])
            w_in = scratch[:, :, :].rearrange("p a (b k n) -> p (a b) k n", b=2, k=KB)
            kT = scratch[:, 0, :].rearrange("p (k n) -> p k n", k=KB)
            v_tok = scratch[:, 1, :].rearrange("p (t d) -> p t d", t=GT)
            att = scratch[:, 2, :].rearrange("p (t d) -> p t d", t=GT)
            w_hi = asb("w_hi", [P, 6, KB, D], F32R)
            w_lo = asb("w_lo", [P, 6, KB, D], F32R)
            bias_rows = asb("bias_rows", [5 * KB, P])
            bias_col = asb("bias_col", [P, 5 * KB])
            b2v_rows = asb("b2v_rows", [P, D])
            lnw_rows = asb("lnw_rows", [P, D])
            lnb_rows = asb("lnb_rows", [P, D])
            causal = asb("causal", [P, GT, P])
            keep = asb("keep", [P, GROUPS])
            x_in = asb("x_in", [P, GT, D])
            xT_hi = asb("xT_hi", [P, KB, GTOK], F32R)
            xT_lo = asb("xT_lo", [P, KB, GTOK], F32R)
            h = asb("h", [P, 2, GTOK])
            zeros = h[:, 0, :]
            h_hi = asb("h_hi", [P, 3, KB, GTOK], F32R)
            h_lo = asb("h_lo", [P, 3, KB, GTOK], F32R)
            q_hi = asb("q_hi", [P, KB, GTOK], F32R)
            q_lo = asb("q_lo", [P, KB, GTOK], F32R)
            k_hi = asb("k_hi", [P, KB, GTOK], F32R)
            k_lo = asb("k_lo", [P, KB, GTOK], F32R)
            v_hi = asb("v_hi", [P, GT, D], F32R)
            v_lo = asb("v_lo", [P, GT, D], F32R)
            ktok_hi = asb("ktok_hi", [P, GT, D], F32R)
            ktok_lo = asb("ktok_lo", [P, GT, D], F32R)
            masked = asb("masked", [P, GT, P])
            masked_hi = asb("masked_hi", [P, GT, P], F32R)
            masked_lo = asb("masked_lo", [P, GT, P], F32R)
            state_hi = asb("state_hi", [P, KB, D], F32R)
            state_lo = asb("state_lo", [P, KB, D], F32R)
            st_o = asb("st_o", [P, GT, 6])
            mv_o = asb("mv_o", [P, GT, 2])
            rs_o = asb("rs_o", [P, GT])
            st_z = asb("st_z", [P, GT, 6])
            mv_z = asb("mv_z", [P, GT, 2])
            ve_o = asb("ve_o", [P, GT])
            ve_z = asb("ve_z", [P, 2, GT])
            r_z = asb("r_z", [P, 2, GT])
            vinv = asb("vinv", [P, GT])
            warm = asb("warm", [P, GT])
            var_x1 = asb("var_x1", [P, GT])
            minus_half = asb("minus_half", [P, 2, GT])

            mu_in = asb("mu_in", [P, KB, ES])
            mu_unit = asb("mu_unit", [P, KB, ES])
            mu_sq = mu_unit
            mu_n2 = asb("mu_n2", [P, SB])
            mu_inv = asb("mu_inv", [P, SB])
            mu_fac = asb("mu_fac", [P, SB])
            mu_diag = asb("mu_diag", [P, SB, P])
            ones = asb("ones", [P, P])
            b1_row = asb("b1_row", [E, P])
            b2_row = asb("b2_row", [E, D])

            moe_loaded = asem("moe_loaded")
            b1_blank = asem("b1_blank")
            mu_squared = asem("mu_squared")
            mu_summed = asem("mu_summed")
            mu_floored = asem("mu_floored")
            mu_rs = asem("mu_rs")
            mu_scaled = asem("mu_scaled")
            mu_spread = asem("mu_spread")
            mu_rows = asem("mu_rows")
            mu_united = asem("mu_united")
            mu_rounded = asem("mu_rounded")
            mu_ready = asem("mu_ready")
            scale_neg = asem("scale_neg")
            shift_ready = asem("shift_ready")
            moe_turned = asem("moe_turned")
            moe_ready = asem("moe_ready")
            x_loaded = asem("x_loaded")
            weight_loaded = [asem(f"weight_loaded{n}") for n in range(6)]
            bias_loaded = asem("bias_loaded")
            rows_loaded = asem("rows_loaded")
            table_warm = asem("table_warm")
            ident_blank = asem("ident_blank")
            masks_ready = asem("masks_ready")
            keep_blank = asem("keep_blank")
            keep_ready = asem("keep_ready")
            w_rounded = asem("w_rounded")
            w_split = asem("w_split")
            bias_turned = asem("bias_turned")
            bias_ready = asem("bias_ready")
            xT_done = asem("xT_done")
            x_rounded = asem("x_rounded")
            x_split = asem("x_split")
            hidden_done = asem("hidden_done")
            h_rounded = asem("h_rounded")
            hqk_split = asem("hqk_split")
            hv_split = asem("hv_split")
            qk_done = asem("qk_done")
            q_rounded = asem("q_rounded")
            q_split = asem("q_split")
            k_rounded = asem("k_rounded")
            k_split = asem("k_split")
            v_done = asem("v_done")
            v_biased = asem("v_biased")
            v_rounded = asem("v_rounded")
            v_split0 = asem("v_split0")
            v_split1 = asem("v_split1")
            kt_done = asem("kt_done")
            ktok_rounded = asem("ktok_rounded")
            ktok_split = asem("ktok_split")
            scores_done = asem("scores_done")
            scores_masked = asem("scores_masked")
            masked_rounded = asem("masked_rounded")
            masked_split = asem("masked_split")
            state_updated = asem("state_updated")
            state_gated = asem("state_gated")
            state_rounded = asem("state_rounded")
            state_split = asem("state_split")
            chunk_done = asem("chunk_done")
            chunk_mv = asem("chunk_mv")
            chunk_ve = asem("chunk_ve")
            chunk_rs = asem("chunk_rs")
            chunk_normed = asem("chunk_normed")
            xb_ready = asem("xb_ready")
            att_weighted = asem("att_weighted")
            z_ready = asem("z_ready")
            z_mv = asem("z_mv")
            z_ve = asem("z_ve")
            z_vinv = asem("z_vinv")
            x1_var = asem("x1_var")
            x1_ve = asem("x1_ve")
            z_rs = asem("z_rs")
            x1_ready = asem("x1_ready")
            r2_ready = asem("r2_ready")

            XT0, XT1, Q1, K1, V1, Q2, K2, V2, KT = 0, 1, 2, 4, 6, 8, 10, 12, 14
            scores_ps, state_ps, chunk_ps = bank[4], bank[5], [bank[6], bank[7]]
            LAYERS = {"q": 0, "k": 1, "v": 2}

            def job_bank(job):
                return bank[job % 4]

            def run_groups(body, engine, after_first, before_last):
                body(0, attend=False)
                after_first()
                with engine.Fori(1, GROUPS) as g:
                    body(g, attend=True)
                before_last()
                body(GROUPS, attend=True, project=False)

            block = attn.enter_context(nc.Block())

            @block.sync
            def _(sp):
                def load_x(g):
                    sp.dma_start(x_in[:, :, :], x_t[:, bass.ds(g * GT, GT), :]).then_inc(x_loaded, 16)

                load_x(0)
                for n, w in enumerate((W1q, W1k, W1v, W2q, W2k, W2v)):
                    sp.dma_start(w_in[:, n, :, :], w.rearrange("(k p) n -> p k n", p=P)).then_inc(weight_loaded[n], 16)
                for src, tile in ((b2v, b2v_rows), (ln_b, lnb_rows), (ln_w, lnw_rows)):
                    sp.dma_start(tile[:, :], src.partition_broadcast(P)).then_inc(rows_loaded, 16)
                for src, tile in ((gamma, g_rows), (beta, b_rows), (scale, scale_col)):
                    sp.dma_start(tile[:, :], src.partition_broadcast(P)).then_inc(moe_loaded, 16)
                sp.dma_start(mu_in[:, :, :], mu.rearrange("(k p) e s -> p k (e s)", p=P)).then_inc(moe_loaded, 16)
                sp.dma_start(b2_row[:, :], b2).then_inc(moe_loaded, 16)
                sp.wait_ge(b1_blank, 1)
                sp.dma_start(b1_row[:, 0:H], b1).then_inc(moe_loaded, 16)
                with sp.Fori(1, GROUPS) as g:
                    sp.wait_ge(xT_done, 2 * g)
                    sp.wait_ge(xb_ready, g)
                    load_x(g)

            @block.gpsimd
            def _(pool):
                pool.memset(ident[:, :], 0.0)
                pool.memset(causal[:, :, :], 1.0)
                pool.memset(keep[:, :], 1.0)
                pool.memset(minus_half[:, :, :], -0.5)
                pool.memset(ones[:, :], 1.0)
                pool.memset(b1_row[:, :], 0.0).then_inc(b1_blank, 1)
                pool.memset(zeros, 0.0).then_inc(ident_blank, 1)
                pool.wait_ge(ident_blank, 1)
                pool.affine_select(out=ident[:, :], in_=ident[:, :], compare_op=ALU.not_equal, fill=1.0,
                                   base=0, pattern=[[-1, P]], channel_multiplier=1)
                pool.affine_select(out=causal[:, :, :], in_=causal[:, :, :], compare_op=ALU.is_ge, fill=0.0,
                                   base=0, pattern=[[0, GT], [1, P]], channel_multiplier=-1)
                pool.memset(keep[:, :].rearrange("p (b g) -> p b g", g=GB)[:, :, 0:1], 0.0).then_inc(masks_ready, 1)

                def split_hv(g):
                    for m in range(2):
                        pool.wait_ge(h_rounded, 6 * g + 4 + m + 1)
                        pool.tensor_tensor(h_lo[:, 2, m, :], h[:, m, :], h_hi[:, 2, m, :].bitcast(F32),
                                           ALU.subtract).then_inc(hv_split, 1)

                def add_ln_b(g):
                    pool.wait_ge(x_loaded, 16 * (g + 1))
                    if isinstance(g, int) and g == 0:
                        pool.wait_ge(rows_loaded, 16 * 3)
                    pool.tensor_tensor(x1_all[:, bass.ds(g * GT, GT), :], x_in[:, :, :],
                                       lnb_rows[:, :].unsqueeze(1).to_broadcast([P, GT, D]),
                                       ALU.add).then_inc(xb_ready, 1)

                def body(g, attend, project=True):
                    if attend:
                        a = g - 1
                        for c in range(GT):
                            n = GT * a + c
                            pool.wait_ge(chunk_ve, n + 1)
                            pool.tensor_tensor(rs_o[:, c:c + 1], ve_o[:, c:c + 1], minus_half[:, 0, 0:1],
                                               ALU.pow).then_inc(chunk_rs, 1)
                            if project and c == 0:
                                add_ln_b(g)
                            pool.wait_ge(chunk_normed, n + 1 + 2)
                            pool.tensor_tensor(att[:, c, :], att[:, c, :], lnw_rows[:, :],
                                               ALU.mult).then_inc(att_weighted, 1)
                            pool.wait_ge(att_weighted, n + 1)
                            z = x1_all[:, bass.ds(n, 1), :]
                            pool.tensor_tensor(z, z, att[:, c:c + 1, :], ALU.add).then_inc(z_ready, 1)
                            if project and c == 2:
                                split_hv(g)
                    else:
                        add_ln_b(g)
                        split_hv(g)
                    if project:
                        split_v(g, 1)
                    if attend:
                        pool.wait_ge(x1_ve, a + 1)
                        pool.tensor_tensor(r_z[:, :, :], ve_z[:, :, :], minus_half[:, :, :],
                                           ALU.pow).then_inc(z_rs, 1)

                def split_v(g, m):
                    pool.wait_ge(v_rounded, 2 * g + m + 1)
                    pair = slice(2 * m, 2 * m + 2)
                    pool.tensor_tensor(v_lo[:, pair, :], v_tok[:, pair, :], v_hi[:, pair, :].bitcast(F32),
                                       ALU.subtract).then_inc(v_split1, 1)

                def invert_mu_norms():
                    pool.wait_ge(mu_floored, 1)
                    pool.tensor_tensor(mu_inv[:, :], mu_n2[:, :], minus_half[:, 0, 0:SB], ALU.pow).then_inc(mu_rs, 1)

                run_groups(body, pool, invert_mu_norms, lambda: None)

            @block.scalar
            def _(act):
                rows = ((b1q, 0), (b1k, 1), (b1v, 2), (b2q, 3), (b2k, 4))
                for b_row, n in rows:
                    act.dma_start(bias_rows[KB * n:KB * n + KB, :],
                                  b_row.rearrange("(k p) -> k p", p=P)).then_inc(bias_loaded, 16)

                def round_state(a, c):
                    act.wait_ge(state_updated, GT * a + c + 1)
                    if c == 0:
                        act.wait_ge(state_gated, a + 1)
                    nc.scalar.copy(state_hi[:, :, :], state_ps[:, :].rearrange("p (k d) -> p k d", k=KB)
                                   ).then_inc(state_rounded, 1)

                def round_x(g, kb):
                    act.wait_ge(xT_done, 2 * g + kb + 1)
                    nc.scalar.copy(xT_hi[:, kb, :], job_bank(XT0 + kb)[:, :]).then_inc(x_rounded, 1)

                def hidden(g, n, m):
                    act.wait_ge(hidden_done, 6 * g + 2 * n + m + 1)
                    if n > 0:
                        act.wait_ge(hqk_split, 4 * g + 2 * (n - 1) + m + 1)
                    elif not (isinstance(g, int) and g == 0):
                        act.wait_ge(hv_split, 2 * g - 1 + m)
                    ps = job_bank(Q1 + 2 * n + m)
                    bias = bias_col[:, KB * n + m:KB * n + m + 1]
                    nc.scalar.activation(h[:, m, :], ps[:, :], ACT.Gelu, bias=bias)
                    nc.scalar.activation(h_hi[:, n, m, :], ps[:, :], ACT.Gelu, bias=bias).then_inc(h_rounded, 1)

                def round_q(g, m):
                    act.wait_ge(qk_done, 4 * g + m + 1)
                    nc.scalar.activation(q_hi[:, m, :], job_bank(Q2 + m)[:, :], ACT.Identity,
                                         bias=bias_col[:, KB * 3 + m:KB * 3 + m + 1]).then_inc(q_rounded, 1)

                def round_k(g, m):
                    act.wait_ge(qk_done, 4 * g + 2 + m + 1)
                    ps = job_bank(K2 + m)
                    bias = bias_col[:, KB * 4 + m:KB * 4 + m + 1]
                    nc.scalar.activation(kT[:, m, :], ps[:, :], ACT.Identity, bias=bias)
                    nc.scalar.activation(k_hi[:, m, :], ps[:, :], ACT.Identity, bias=bias).then_inc(k_rounded, 1)

                def round_v(g, m):
                    act.wait_ge(v_biased, 2 * g + m + 1)
                    pair = slice(2 * m, 2 * m + 2)
                    nc.scalar.copy(v_hi[:, pair, :], v_tok[:, pair, :]).then_inc(v_rounded, 1)

                def round_masked(g):
                    act.wait_ge(scores_masked, g + 1)
                    nc.scalar.copy(masked_hi[:, :, :], masked[:, :, :]).then_inc(masked_rounded, 1)

                def round_ktok(g, m):
                    act.wait_ge(kt_done, 2 * g + m + 1)
                    nc.scalar.copy(ktok_hi[:, 2 * m:2 * m + 2, :],
                                   job_bank(KT + m)[:, :].rearrange("p (t d) -> p t d", t=2)
                                   ).then_inc(ktok_rounded, 1)

                def square_mu():
                    act.wait_ge(moe_loaded, 16 * 6)
                    nc.scalar.activation(mu_sq[:, :, :], mu_in[:, :, :], ACT.Square).then_inc(mu_squared, 1)

                def body(g, attend, project=True):
                    a = g - 1
                    if project:
                        round_x(g, 0)
                        round_x(g, 1)
                    if not attend:
                        act.wait_ge(bias_turned, 1)
                        nc.scalar.copy(bias_col[:, :], bank[7][:, 0:5 * KB]).then_inc(bias_ready, 1)
                        act.wait_ge(bias_ready, 1)
                    for c in range(GT):
                        if attend and c + 1 < GT:
                            round_state(a, c + 1)
                        if project and c < 3:
                            hidden(g, c, 0)
                            hidden(g, c, 1)
                    if not attend:
                        square_mu()
                    if project:
                        round_state(g, 0)
                        for m in range(KB):
                            round_q(g, m)
                        for m in range(KB):
                            round_k(g, m)
                        for m in range(2):
                            round_v(g, m)
                        round_masked(g)
                        for m in range(2):
                            round_ktok(g, m)

                act.wait_ge(z_ready, 1)
                nc.scalar.activation(warm[:, :], vinv[:, :], ACT.Gelu).then_inc(table_warm, 1)

                def copy_moe_biases():
                    act.wait_ge(moe_turned, 1)
                    nc.scalar.copy(b1T[:, :], bank[0][:, 0:E]).then_inc(moe_ready, 1)
                    nc.scalar.copy(b2T[:, :, :], bank[0][:, E:3 * E].rearrange("p (k e) -> p k e", k=KB)
                                   ).then_inc(moe_ready, 1)

                run_groups(body, act, lambda: None, copy_moe_biases)
                act.wait_ge(moe_ready, 2)
                act.wait_ge(table_warm, 1)

            @block.tensor
            def _(pe):
                def split3(ps, w, xs, start, stop):
                    nc.tensor.matmul(ps, w[0], xs[0], start=start, stop=False)
                    nc.tensor.matmul(ps, w[0], xs[1], start=False, stop=False)
                    return nc.tensor.matmul(ps, w[1], xs[0], start=False, stop=stop)

                def turn_x(g, kb):
                    if kb == 0:
                        pe.wait_ge(x_loaded, 16 * (g + 1))
                    if not (isinstance(g, int) and g == 0):
                        pe.wait_ge(v_biased, 2 * g - 1 + kb)
                    for t in range(GT):
                        last = nc.tensor.transpose(job_bank(XT0 + kb)[:, t * P:(t + 1) * P],
                                                   x_in[:, t, kb * P:(kb + 1) * P], ident[:, :])
                    last.then_inc(xT_done, 1)

                def hidden(g, n, m):
                    if n == 0:
                        if m == 0:
                            pe.wait_ge(x_split, 2 * g + 2)
                        if not (isinstance(g, int) and g == 0):
                            pe.wait_ge(ktok_split, 2 * g - 1 + m)
                    if n == 2:
                        pe.wait_ge(h_rounded, 6 * g + m + 1)
                    if isinstance(g, int) and g == 0:
                        pe.wait_ge(w_split, n + 1)
                    for kb in range(KB):
                        cols = slice(m * P, (m + 1) * P)
                        last = split3(job_bank(Q1 + 2 * n + m)[:, :],
                                      (w_hi[:, n, kb, cols], w_lo[:, n, kb, cols]),
                                      (xT_hi[:, kb, :], xT_lo[:, kb, :]), kb == 0, kb == KB - 1)
                    last.then_inc(hidden_done, 1)

                def project_qk(g, n, m):
                    pe.wait_ge(hqk_split, 4 * g + 2 * n + 2)
                    pe.wait_ge(h_rounded, 6 * g + 2 * (n + 1) + m + 1)
                    if isinstance(g, int) and g == 0:
                        pe.wait_ge(w_split, 3 + n + 1)
                    for kb in range(KB):
                        cols = slice(m * P, (m + 1) * P)
                        last = split3(job_bank(Q2 + 2 * n + m)[:, :],
                                      (w_hi[:, 3 + n, kb, cols], w_lo[:, 3 + n, kb, cols]),
                                      (h_hi[:, n, kb, :], h_lo[:, n, kb, :]), kb == 0, kb == KB - 1)
                    last.then_inc(qk_done, 1)

                def project_v(g, m):
                    pe.wait_ge(hv_split, 2 * g + 2)
                    pe.wait_ge(q_split, 2 * g + m + 1)
                    if isinstance(g, int) and g == 0:
                        pe.wait_ge(w_split, 6)
                    for half in range(2):
                        toks = slice((2 * m + half) * P, (2 * m + half + 1) * P)
                        for kb in range(KB):
                            last = split3(job_bank(V2 + m)[:, half * D:(half + 1) * D],
                                          (h_hi[:, 2, kb, toks], h_lo[:, 2, kb, toks]),
                                          (w_hi[:, 5, kb, :], w_lo[:, 5, kb, :]), kb == 0, kb == KB - 1)
                    last.then_inc(v_done, 1)

                def turn_k(g, m):
                    pe.wait_ge(k_rounded, 2 * g + 2)
                    for half in range(2):
                        for kb in range(KB):
                            at = half * D + kb * P
                            last = nc.tensor.transpose(
                                job_bank(KT + m)[:, at:at + P],
                                kT[:, kb, (2 * m + half) * P:(2 * m + half + 1) * P], ident[:, :])
                    last.then_inc(kt_done, 1)

                def scores(g):
                    if not (isinstance(g, int) and g == 0):
                        pe.wait_ge(scores_masked, g)
                    pe.wait_ge(q_split, 2 * g + 2)
                    pe.wait_ge(k_split, 2 * g + 2)
                    for c in range(GT):
                        toks = slice(c * P, (c + 1) * P)
                        for kb in range(KB):
                            last = split3(scores_ps[:, toks], (k_hi[:, kb, toks], k_lo[:, kb, toks]),
                                          (q_hi[:, kb, toks], q_lo[:, kb, toks]), kb == 0, kb == KB - 1)
                    last.then_inc(scores_done, 1)

                def chunk(a, c):
                    toks = slice(c * P, (c + 1) * P)
                    ps = chunk_ps[c % 2][:, 0:D]
                    pe.wait_ge(chunk_normed, GT * a + c + 1)
                    pe.wait_ge(state_split, GT * a + c + 1)
                    for kb in range(KB):
                        split3(ps, (q_hi[:, kb, toks], q_lo[:, kb, toks]),
                               (state_hi[:, kb, :], state_lo[:, kb, :]), kb == 0, False)
                    if c == 0:
                        pe.wait_ge(masked_split, a + 1)
                        pe.wait_ge(v_split0, a + 1)
                    if c == 2:
                        pe.wait_ge(v_split1, a + 1)
                    v = (v_hi[:, c, :], v_lo[:, c, :])
                    split3(ps, (masked_hi[:, c, :], masked_lo[:, c, :]), v, False, True).then_inc(chunk_done, 1)
                    if c % 2 == 0:
                        pe.wait_ge(ktok_split, 2 * a + c // 2 + 1)
                    for kb in range(KB):
                        state = state_ps[:, kb * D:(kb + 1) * D]
                        for w, r in ((ktok_hi, 0), (ktok_hi, 1), (ktok_lo, 0)):
                            last = nc.tensor.matmul(state, w[:, c, kb * P:(kb + 1) * P], v[r], start=False,
                                                    stop=False, skip_group_check=True)
                    last.then_inc(state_updated, 1)

                def turn_biases():
                    pe.wait_ge(bias_loaded, 16 * 5)
                    nc.tensor.transpose(bank[7][:, 0:5 * KB], bias_rows[:, :], ident[0:5 * KB, 0:5 * KB]
                                        ).then_inc(bias_turned, 1)
                    nc.tensor.matmul(state_ps[:, :], ident[:, :], zeros, start=True, stop=True
                                     ).then_inc(state_updated, 1)
                    pe.wait_ge(bias_ready, 1)

                def sum_mu_squares():
                    pe.wait_ge(mu_squared, 1)
                    for sblk in range(SB):
                        for kb in range(KB):
                            last = nc.tensor.matmul(bank[7][:, sblk:sblk + 1], mu_sq[:, kb, sblk * P:(sblk + 1) * P],
                                                    ones[:, 0:1], start=(kb == 0), stop=(kb == KB - 1))
                    last.then_inc(mu_summed, 1)

                def body(g, attend, project=True):
                    a = g - 1
                    if project:
                        turn_x(g, 0)
                        turn_x(g, 1)
                    if not attend:
                        turn_biases()
                    for c in range(GT):
                        if attend:
                            chunk(a, c)
                        if project and c < 3:
                            hidden(g, c, 0)
                            hidden(g, c, 1)
                    if project:
                        for n in range(2):
                            project_qk(g, n, 0)
                            project_qk(g, n, 1)
                        project_v(g, 0)
                        project_v(g, 1)
                        if not attend:
                            sum_mu_squares()
                        scores(g)
                        turn_k(g, 0)
                        turn_k(g, 1)

                def turn_moe_rows():
                    pe.wait_ge(moe_loaded, 16 * 6)
                    pe.wait_ge(v_biased, 2 * GROUPS)
                    nc.tensor.transpose(bank[0][:, 0:E], b1_row[:, :], ident[0:E, 0:E])
                    for kb in range(KB):
                        last = nc.tensor.transpose(bank[0][:, (1 + kb) * E:(2 + kb) * E],
                                                   b2_row[:, kb * P:(kb + 1) * P], ident[0:E, 0:E])
                    last.then_inc(moe_turned, 1)
                    pe.wait_ge(mu_spread, SB)
                    for sblk in range(SB):
                        last = nc.tensor.matmul(bank[1][:, sblk * P:(sblk + 1) * P], ones[:, :], mu_diag[:, sblk, :],
                                                start=True, stop=True)
                    last.then_inc(mu_rows, 1)

                pe.wait_ge(masks_ready, 1)
                run_groups(body, pe, lambda: pe.wait_ge(mu_floored, 1),
                           turn_moe_rows)

            @block.vector
            def _(dve):
                nc.vector.memset(rs_o[:, :], 0.0).then_inc(chunk_normed, 2)
                nc.vector.memset(vinv[:, :], 0.0).then_inc(z_ready, 1)

                def split_weight(n):
                    dve.wait_ge(weight_loaded[n], 16)
                    nc.vector.tensor_copy(w_hi[:, n, :, :], w_in[:, n, :, :]).then_inc(w_rounded, 1)
                    dve.wait_ge(w_rounded, n + 1)
                    nc.vector.tensor_tensor(w_lo[:, n, :, :], w_in[:, n, :, :], w_hi[:, n, :, :].bitcast(F32),
                                            ALU.subtract).then_inc(w_split, 1)

                def gate_state(a):
                    dve.wait_ge(state_updated, GT * a + 1)
                    nc.vector.tensor_scalar(state_ps[:, :], state_ps[:, :], keep[:, bass.ds(a, 1)], None,
                                            ALU.mult).then_inc(state_gated, 1)

                def mask_scores(a):
                    dve.wait_ge(scores_done, a + 1)
                    nc.vector.tensor_tensor(masked[:, :, :], scores_ps[:, :].rearrange("p (c n) -> p c n", c=GT),
                                            causal[:, :, :], ALU.mult).then_inc(scores_masked, 1)

                def split_x(g, kb):
                    dve.wait_ge(x_rounded, 2 * g + kb + 1)
                    nc.vector.tensor_tensor(xT_lo[:, kb, :], job_bank(XT0 + kb)[:, :],
                                            xT_hi[:, kb, :].bitcast(F32), ALU.subtract).then_inc(x_split, 1)

                def split_state(a, c):
                    dve.wait_ge(state_rounded, GT * a + c + 1)
                    nc.vector.tensor_tensor(state_lo[:, :, :], state_ps[:, :].rearrange("p (k d) -> p k d", k=KB),
                                            state_hi[:, :, :].bitcast(F32), ALU.subtract).then_inc(state_split, 1)

                def split_masked(g):
                    dve.wait_ge(masked_rounded, g + 1)
                    nc.vector.tensor_tensor(masked_lo[:, :, :], masked[:, :, :], masked_hi[:, :, :].bitcast(F32),
                                            ALU.subtract).then_inc(masked_split, 1)

                def split_q(g, m):
                    dve.wait_ge(q_rounded, 2 * g + m + 1)
                    nc.vector.scalar_tensor_tensor(
                        out=q_lo[:, m, :], in0=job_bank(Q2 + m)[:, :], scalar=bias_col[:, KB * 3 + m:KB * 3 + m + 1],
                        in1=q_hi[:, m, :].bitcast(F32), op0=ALU.add, op1=ALU.subtract).then_inc(q_split, 1)

                def split_k(g, m):
                    dve.wait_ge(k_rounded, 2 * g + m + 1)
                    nc.vector.tensor_tensor(k_lo[:, m, :], kT[:, m, :], k_hi[:, m, :].bitcast(F32),
                                            ALU.subtract).then_inc(k_split, 1)

                def split_ktok(g, m):
                    dve.wait_ge(ktok_rounded, 2 * g + m + 1)
                    pair = slice(2 * m, 2 * m + 2)
                    nc.vector.tensor_tensor(ktok_lo[:, pair, :],
                                            job_bank(KT + m)[:, :].rearrange("p (t d) -> p t d", t=2),
                                            ktok_hi[:, pair, :].bitcast(F32), ALU.subtract).then_inc(ktok_split, 1)

                def split_h(g, n, m):
                    dve.wait_ge(h_rounded, 6 * g + 2 * n + m + 1)
                    nc.vector.tensor_tensor(h_lo[:, n, m, :], h[:, m, :], h_hi[:, n, m, :].bitcast(F32),
                                            ALU.subtract).then_inc(hqk_split, 1)

                def bias_v(g, m):
                    dve.wait_ge(v_done, 2 * g + m + 1)
                    nc.vector.tensor_tensor(v_tok[:, 2 * m:2 * m + 2, :],
                                            job_bank(V2 + m)[:, :].rearrange("p (t d) -> p t d", t=2),
                                            b2v_rows[:, :].unsqueeze(1).to_broadcast([P, 2, D]),
                                            ALU.add).then_inc(v_biased, 1)

                def split_v(g, m):
                    dve.wait_ge(v_rounded, 2 * g + m + 1)
                    pair = slice(2 * m, 2 * m + 2)
                    nc.vector.tensor_tensor(v_lo[:, pair, :], v_tok[:, pair, :], v_hi[:, pair, :].bitcast(F32),
                                            ALU.subtract).then_inc(v_split0, 1)

                def chunk_statistics(a, c):
                    n = GT * a + c
                    dve.wait_ge(chunk_done, n + 1)
                    nc.vector.bn_stats(st_o[:, c, :], chunk_ps[c % 2][:, 0:D])
                    dve.drain()
                    nc.vector.bn_aggr(mv_o[:, c, :], st_o[:, c, :]).then_inc(chunk_mv, 1)
                    dve.wait_ge(chunk_mv, n + 1)
                    nc.vector.tensor_scalar(ve_o[:, c:c + 1], mv_o[:, c, 1:2], LN_EPS * SCORE_DIV2, None,
                                            ALU.add).then_inc(chunk_ve, 1)

                def norm_chunk(a, c):
                    n = GT * a + c
                    dve.wait_ge(chunk_rs, n + 1)
                    if c == 0:
                        dve.wait_ge(z_ready, GT * a + 1)
                    nc.vector.tensor_scalar(att[:, c, :], chunk_ps[c % 2][:, 0:D], mv_o[:, c, 0:1],
                                            rs_o[:, c:c + 1], ALU.subtract, ALU.mult).then_inc(chunk_normed, 1)

                def z_statistics(a, c):
                    n = GT * a + c
                    dve.wait_ge(z_ready, n + 2)
                    nc.vector.bn_stats(st_z[:, c, :], x1_all[:, bass.ds(n, 1), :])
                    dve.drain()
                    nc.vector.bn_aggr(mv_z[:, c, :], st_z[:, c, :]).then_inc(z_mv, 1)

                def norm_z(a):
                    var = mv_z[:, :, 1]
                    dve.wait_ge(z_mv, GT * a + GT)
                    nc.vector.tensor_scalar(ve_z[:, 0, :], var, LN_EPS, None, ALU.add).then_inc(z_ve, 1)
                    dve.wait_ge(z_ve, a + 1)
                    nc.vector.reciprocal(vinv[:, :], ve_z[:, 0, :]).then_inc(z_vinv, 1)
                    dve.wait_ge(z_vinv, a + 1)
                    nc.vector.tensor_tensor(var_x1[:, :], var, vinv[:, :], ALU.mult).then_inc(x1_var, 1)
                    dve.wait_ge(x1_var, a + 1)
                    nc.vector.tensor_scalar(ve_z[:, 1, :], var_x1[:, :], LN_EPS, None, ALU.add).then_inc(x1_ve, 1)

                def apply_z(a):
                    dve.wait_ge(z_rs, a + 1)
                    for c in range(GT):
                        xc = x1_all[:, bass.ds(GT * a + c, 1), :]
                        nc.vector.tensor_scalar(xc, xc, mv_z[:, c, 0:1], r_z[:, 0, c:c + 1],
                                                ALU.subtract, ALU.mult).then_inc(x1_ready, 1)
                    nc.vector.tensor_copy(r2_all[:, bass.ds(GT * a, GT)], r_z[:, 1, :]).then_inc(r2_ready, 1)

                def floor_mu():
                    dve.wait_ge(mu_summed, 1)
                    nc.vector.tensor_scalar(mu_n2[:, :], bank[7][:, 0:SB], NORM_EPS ** 2, None, ALU.max
                                            ).then_inc(mu_floored, 1)

                def body(g, attend, project=True, more=True):
                    a = g - 1
                    for c in range(GT):
                        if attend and c + 1 < GT:
                            split_state(a, c + 1)
                        if attend and c > 1:
                            z_statistics(a, c - 2)
                        if attend:
                            chunk_statistics(a, c)
                        if project and c < 2:
                            split_h(g, c, 0)
                            split_h(g, c, 1)
                        if attend and c < GT - 1:
                            norm_chunk(a, c)
                    if project:
                        gate_state(g)
                        split_state(g, 0)
                        split_q(g, 0)
                        split_q(g, 1)
                    if attend:
                        norm_chunk(a, GT - 1)
                        z_statistics(a, GT - 2)
                    if project:
                        split_k(g, 0)
                        split_k(g, 1)
                        bias_v(g, 0)
                    if attend:
                        z_statistics(a, GT - 1)
                    if project:
                        bias_v(g, 1)
                        split_v(g, 0)
                        if not attend:
                            floor_mu()
                        mask_scores(g)
                    if attend:
                        norm_z(a)
                    if project:
                        split_masked(g)
                        split_ktok(g, 0)
                        if more:
                            split_x(g + 1, 0)
                            split_x(g + 1, 1)
                        split_ktok(g, 1)
                    if attend:
                        apply_z(a)

                def mu_factors():
                    nc.vector.tensor_scalar(shift[:, :], scale_col[:, :], -1.0, None, ALU.mult).then_inc(scale_neg, 1)
                    dve.wait_ge(scale_neg, 1)
                    nc.vector.tensor_tensor(shift[:, :], shift[:, :], scale_col[:, :], ALU.min).then_inc(shift_ready, 1)
                    dve.wait_ge(mu_rs, 1)
                    nc.vector.tensor_scalar(mu_fac[:, :], mu_inv[:, :], scale_col[:, :], None,
                                            ALU.mult).then_inc(mu_scaled, 1)
                    dve.wait_ge(mu_scaled, 1)
                    for sblk in range(SB):
                        nc.vector.tensor_scalar(mu_diag[:, sblk, :], ident[:, :], mu_fac[:, sblk:sblk + 1], None,
                                                ALU.mult).then_inc(mu_spread, 1)

                def mu_units():
                    dve.wait_ge(mu_rows, 1)
                    nc.vector.tensor_tensor(mu_unit[:, :, :], mu_in[:, :, :],
                                            bank[1][:, 0:ES].unsqueeze(1).to_broadcast([P, KB, ES]),
                                            ALU.mult).then_inc(mu_united, 1)
                    dve.wait_ge(mu_united, 1)
                    nc.vector.tensor_copy(mu_hi[:, :, :], mu_unit[:, :, :]).then_inc(mu_rounded, 1)
                    dve.wait_ge(mu_rounded, 1)
                    nc.vector.tensor_tensor(mu_lo[:, :, :], mu_unit[:, :, :], mu_hi[:, :, :].bitcast(F32),
                                            ALU.subtract).then_inc(mu_ready, 1)

                split_weight(0)
                split_x(0, 0)
                split_x(0, 1)
                for n in range(1, 6):
                    split_weight(n)
                dve.wait_ge(masks_ready, 1)
                dve.wait_ge(rows_loaded, 16 * 3)
                body(0, attend=False, more=False)
                split_x(1, 0)
                split_x(1, 1)
                mu_factors()
                with dve.Fori(1, GROUPS - 1) as g:
                    body(g, attend=True)
                body(GROUPS - 1, attend=True, more=False)
                mu_units()
                body(GROUPS, attend=True, project=False)
                dve.wait_ge(x1_ready, TILES)
                dve.wait_ge(r2_ready, GROUPS)
                dve.wait_ge(shift_ready, 1)
                dve.wait_ge(mu_ready, 1)

        with ExitStack() as moe:
            def msb(name, shape, dt=F32):
                return sb(name, shape, dt, moe)

            def msem(name):
                return sem(name, moe)

            ET_all = msb("ET_all", [P, SB, TILES * P])
            rsum = msb("rsum", [P, TILES])
            rinv = msb("rinv", [P, TILES])
            xn_all = msb("xn_all", [P, GB * GT * (D + 1)])
            xn = [xn_all[:, q * GT * (D + 1):(q + 1) * GT * (D + 1)].rearrange("p (t d) -> p t d", t=GT)
                  for q in range(GB)]
            xnT_hi = [msb(f"xnT_hi{q}", [P, KB, GTOK], F32R) for q in range(2)]
            xnT_lo = [msb(f"xnT_lo{q}", [P, KB, GTOK], F32R) for q in range(2)]
            square = msb("square", [P, 2, D])
            n2 = msb("n2", [P, GB, GT])
            n2_low = msb("n2_low", [P, GB, GT])
            xinv = msb("xinv", [P, GB, GT])
            minus_half = msb("minus_half2", [P, GT])
            blank = msb("blank", [P, 12])
            e_tok = msb("e_tok", [P, 4, ES])
            colinv = msb("colinv", [P, SB])
            slot_in = msb("slot_in", [P, SB, D])
            slot_inT = msb("slot_inT", [P, KB, B, ES])
            w1_sb = msb("w1_sb", [P, KB, E, H])

            w1_loaded = msem("w1_loaded")
            w2_loaded = msem("w2_loaded")
            half_set = msem("half_set")
            ones_set = msem("ones_set")
            tok_scaled = msem("tok_scaled")
            xn_ready = msem("xn_ready")
            n2_ready = msem("n2_ready")
            n2_floored = msem("n2_floored")
            xinv_ready = msem("xinv_ready")
            xnT_done = msem("xnT_done")
            xnT_rounded = msem("xnT_rounded")
            xnT_split = msem("xnT_split")
            logits_done = msem("logits_done")
            e_ready = msem("e_ready")
            eT_done = msem("eT_done")
            eT_ready = msem("eT_ready")
            tile_folded = msem("tile_folded")
            rinv_ready = msem("rinv_ready")
            colinv_ready = msem("colinv_ready")
            slot_in_ready = msem("slot_in_ready")
            slot_in_turned = msem("slot_in_turned")
            slot_inT_ready = msem("slot_inT_ready")

            xnT_ps, log_ps, eT_ps, fold_ps = bank[0:2], bank[2:4], bank[4:6], bank[6:8]
            slotT_ps = fold_ps[0]
            LEAD = 2

            w2_sb = xn_all[0:H, 0:E * D].rearrange("h (e d) -> h e d", e=E)
            hs = e_tok[0:H, :, :].rearrange("p i (e n) -> p (i e) n", n=B * S)
            soT = slot_inT
            so = w1_sb[:, :, :, :].rearrange("p k (b e) (s h) -> p (k b) (e s h)", b=2, s=1
                                             ).rearrange("p b (s d) -> p b s d", s=SB)
            hs_done = msem("hs_done")
            hs_biased = msem("hs_biased")
            hs_ready = msem("hs_ready")
            soT_done = msem("soT_done")
            soT_ready = msem("soT_ready")
            so_done = msem("so_done")
            so_ready = msem("so_ready")

            eT_flat = slot_inT[:, :, :, :].rearrange("p k b s -> p (k b s)")
            eT = [eT_flat[:, q * SB * GTOK:(q + 1) * SB * GTOK].rearrange("p (s n) -> p s n", s=SB) for q in range(2)]
            y = xn
            st_y = msb("st_y", [P, GT, 6])
            mv_y = msb("mv_y", [P, 2, GT, 2])
            ve_y = msb("ve_y", [P, 2, GT])
            rs_y = msb("rs_y", [P, 2, GT])
            eT_staged = msem("eT_staged")
            mixed = msem("mixed")
            mix_scaled = msem("mix_scaled")
            y_ready = msem("y_ready")
            y_mv = msem("y_mv")
            y_ve = msem("y_ve")
            y_rs = msem("y_rs")
            y_normed = msem("y_normed")
            stored = [msem(f"stored{q}") for q in range(GB)]
            mix_ps = bank[0:4]

            block = moe.enter_context(nc.Block())

            @block.sync
            def _(sp):
                for kb in range(KB):
                    sp.dma_start(w1_sb[:, kb, :, :], w1[:, kb * P:(kb + 1) * P, :].rearrange("e p h -> p e h")
                                 ).then_inc(w1_loaded, 16)
                sp.wait_ge(tile_folded, TILES + TB)
                sp.dma_start(w2_sb[:, :, :], w2.rearrange("e h d -> h e d")).then_inc(w2_loaded, 16)
                with sp.Fori(0, B) as b:
                    for q in range(GB):
                        k = GB * b + q
                        sp.wait_ge(y_normed, GT * k + GT)
                        sp.dma_start(out_t[:, bass.ds(GT * k, GT), :], y[q][:, :, 0:D]).then_inc(stored[q], 16)
                for q in range(GB):
                    sp.wait_ge(stored[q], 16 * B + 16)

            @block.gpsimd
            def _(pool):
                for n, (starts, at) in enumerate(((tile_folded, TB), (n2_ready, 1), (e_ready, 2), (eT_ready, 2),
                                                  (slot_inT_ready, 1), (mixed, 2 * GT),
                                                  (mix_scaled, GT), *((stored[q], 16) for q in range(GB)))):
                    pool.memset(blank[:, n:n + 1], 0.0).then_inc(starts, at)
                for q in range(GB):
                    pool.memset(xn[q][:, :, D:D + 1], 1.0).then_inc(ones_set, 1)
                pool.memset(minus_half[:, :], -0.5).then_inc(half_set, 1)
                pool.wait_ge(half_set, 1)

                def invert_norms(k, q):
                    pool.wait_ge(n2_floored, k + 1)
                    pool.tensor_tensor(xinv[:, q, :], n2_low[:, q, :], minus_half[:, :],
                                       ALU.pow).then_inc(xinv_ready, 1)

                def add_beta(k, q):
                    pool.wait_ge(tok_scaled, GT * k + GT)
                    pool.tensor_tensor(xn[q][:, :, 0:D], xn[q][:, :, 0:D],
                                       b_rows[:, :].unsqueeze(1).to_broadcast([P, GT, D]),
                                       ALU.add).then_inc(xn_ready, 1)

                def route(b, last):
                    for q in range(GB):
                        if not (last and q == GB - 1):
                            invert_norms(GB * b + q + 1, (q + 1) % GB)
                        if not (last and q >= GB - 3):
                            add_beta(GB * b + q + 3, (q + 3) % GB)

                add_beta(0, 0)
                add_beta(1, 1)
                invert_norms(0, 0)
                add_beta(2, 2)
                with pool.Fori(0, B - 1) as b:
                    route(b, last=False)
                route(B - 1, last=True)

                def add_residual(k, q):
                    pool.wait_ge(mix_scaled, GT * k + GT + 4)
                    yq = y[q][:, :, 0:D]
                    pool.tensor_tensor(yq, yq, x1_all[:, bass.ds(GT * k, GT), :], ALU.add).then_inc(y_ready, 1)

                def invert_deviation(k, q):
                    pool.wait_ge(y_ve, k + 1)
                    pool.tensor_tensor(rs_y[:, q % 2, :], ve_y[:, q % 2, :], minus_half[:, :], ALU.pow).then_inc(y_rs, 1)

                def finish(b, last):
                    for q in range(GB):
                        if not (last and q == GB - 1):
                            add_residual(GB * b + q + 1, (q + 1) % GB)
                        invert_deviation(GB * b + q, q)

                add_residual(0, 0)
                with pool.Fori(0, B - 1) as b:
                    finish(b, last=False)
                finish(B - 1, last=True)

            @block.scalar
            def _(act):
                def norms(k, q, tiles):
                    act.wait_ge(xn_ready, k + 1)
                    for t in tiles:
                        act.wait_ge(n2_ready, GT * k + max(t - 1, 0) + 1)
                        nc.scalar.activation(square[:, t % 2, :], xn[q][:, t, 0:D], ACT.Square,
                                             accum_out=n2[:, q, t:t + 1]).then_inc(n2_ready, 1)

                def round_xnT(k, q):
                    act.wait_ge(xnT_done, k + 1)
                    for kb in range(KB):
                        nc.scalar.copy(xnT_hi[q % 2][:, kb, :], xnT_ps[kb][:, :]).then_inc(xnT_rounded, 1)

                def exps(b, t):
                    q = t // GT % GB
                    act.wait_ge(logits_done, TB * b + t + 1)
                    act.wait_ge(xinv_ready, GB * b + t // GT + 1)
                    nc.scalar.activation(e_tok[:, t % 4, :], log_ps[t % 2][:, 0:ES], ACT.Exp, bias=shift[:, :],
                                         scale=xinv[:, q, t % GT:t % GT + 1],
                                         accum_out=rsum[:, bass.ds(TB * b + t, 1)]).then_inc(e_ready, 1)

                def step(b, t, last):
                    exps(b, t)
                    k, q = GB * b + t // GT + 1, (t // GT + 1) % GB
                    if not (last and q == 0):
                        if t % GT == 0:
                            norms(k, q, (0, 1))
                        if t % GT == 1:
                            round_xnT(k, q)
                        if t % GT == 2:
                            norms(k, q, (2, 3))

                def route(b, last):
                    for t in range(LEAD, TB + (0 if last else LEAD)):
                        step(b, t, last)
                    act.wait_ge(slot_in_turned, b + 1)
                    nc.scalar.copy(slot_inT[:, :, bass.ds(b, 1), :],
                                   slotT_ps[:, :].rearrange("p (k o n) -> p k o n", k=KB, o=1)
                                   ).then_inc(slot_inT_ready, 1)

                norms(0, 0, range(GT))
                round_xnT(0, 0)
                for t in range(LEAD):
                    step(0, t, last=False)
                with act.Fori(0, B - 1) as b:
                    route(b, last=False)
                route(B - 1, last=True)
                for half in range(2):
                    act.wait_ge(hs_biased, half + 1)
                    eh = slice(half * E // 2, (half + 1) * E // 2)
                    nc.scalar.activation(hs[:, eh, :], hs[:, eh, :], ACT.Gelu).then_inc(hs_ready, 1)
                for n in range(4):
                    act.wait_ge(so_done, n + 1)
                    nc.scalar.copy(so[:, n, :, :], bank[(6, 7, 0, 1)[n]][:, :].rearrange("p (s d) -> p s d", s=SB)
                                   ).then_inc(so_ready, 1)

                def stage_eT(k, q):
                    act.wait_ge(mixed, GT * k + GT)
                    nc.scalar.copy(eT[q % 2][:, :, :], ET_all[:, :, bass.ds(k * GTOK, GTOK)]
                                   ).then_inc(eT_staged, 1)

                def scale_mix(b, q):
                    k = GB * b + q
                    act.wait_ge(stored[q], 16 * b + 16)
                    for t in range(GT):
                        act.wait_ge(mixed, GT * k + t + 1 + 2 * GT)
                        nc.scalar.activation(y[q][:, t, 0:D], mix_ps[t][:, 0:D], ACT.Copy,
                                             scale=rinv[:, bass.ds(GT * k + t, 1)]).then_inc(mix_scaled, 1)

                def combine(b, last):
                    for q in range(GB):
                        if not (last and q == GB - 1):
                            stage_eT(GB * b + q + 1, (q + 1) % GB)
                        scale_mix(b, q)

                act.wait_ge(eT_ready, TILES + 2)
                act.wait_ge(rinv_ready, B)
                stage_eT(0, 0)
                with act.Fori(0, B - 1) as b:
                    combine(b, last=False)
                combine(B - 1, last=True)

            @block.tensor
            def _(pe):
                pe.wait_ge(ones_set, GB)

                def turn_xn(k, q):
                    pe.wait_ge(xn_ready, k + 1)
                    if not (isinstance(k, int) and k == 0):
                        pe.wait_ge(xnT_split, KB * k)
                    for kb in range(KB):
                        for t in range(GT):
                            last = nc.tensor.transpose(xnT_ps[kb][:, t * P:(t + 1) * P],
                                                       xn[q][:, t, kb * P:(kb + 1) * P], ident[:, :])
                    last.then_inc(xnT_done, 1)

                def logits(b, t):
                    q = t // GT % GB
                    toks = slice((t % GT) * P, (t % GT + 1) * P)
                    if t % GT == 0:
                        pe.wait_ge(xnT_split, KB * (GB * b + t // GT + 1))
                    pe.wait_ge(e_ready, TB * b + t + 1)
                    ps = log_ps[t % 2][:, 0:ES]
                    for kb in range(KB):
                        hi, lo = xnT_hi[q % 2][:, kb, toks], xnT_lo[q % 2][:, kb, toks]
                        nc.tensor.matmul(ps, hi, mu_hi[:, kb, :], start=(kb == 0), stop=False)
                        nc.tensor.matmul(ps, hi, mu_lo[:, kb, :], start=False, stop=False)
                        last = nc.tensor.matmul(ps, lo, mu_hi[:, kb, :], start=False, stop=(kb == KB - 1))
                    last.then_inc(logits_done, 1)

                def fold(b, t):
                    q = t // GT
                    pe.wait_ge(e_ready, TB * b + t + 3)
                    pe.wait_ge(eT_ready, TB * b + t + 1)
                    for s in range(SB):
                        last = nc.tensor.transpose(eT_ps[t % 2][:, s * P:(s + 1) * P],
                                                   e_tok[:, t % 4, s * P:(s + 1) * P], ident[:, :])
                    last.then_inc(eT_done, 1)
                    if t == 0:
                        pe.wait_ge(slot_inT_ready, b + 1)
                    for s in range(SB):
                        last = nc.tensor.matmul(fold_ps[s][:, 0:D + 1], e_tok[:, t % 4, s * P:(s + 1) * P],
                                                xn[q][:, t % GT, :], start=(t == 0), stop=(t == TB - 1))
                    last.then_inc(tile_folded, 1)

                def lead(b, t, last):
                    logits(b, t)
                    k, q = GB * b + t // GT + 1, (t // GT + 1) % GB
                    if t % GT == 1 and not (last and q == 0):
                        turn_xn(k, q)

                def route(b, last):
                    for t in range(TB):
                        if t < TB - 1 and not (last and t + LEAD >= TB):
                            lead(b, t + LEAD, last)
                        fold(b, t)
                    if not last:
                        lead(b, TB - 1 + LEAD, last)
                    pe.wait_ge(slot_in_ready, SB * b + SB)
                    for db in range(KB):
                        for s in range(SB):
                            at = (db * SB + s) * P
                            done = nc.tensor.transpose(slotT_ps[:, at:at + P],
                                                       slot_in[:, s, db * P:(db + 1) * P], ident[:, :])
                    done.then_inc(slot_in_turned, 1)

                turn_xn(0, 0)
                for t in range(LEAD):
                    lead(0, t, last=False)
                with pe.Fori(0, B - 1) as b:
                    route(b, last=False)
                route(B - 1, last=True)

                pe.wait_ge(w1_loaded, 16 * KB)
                pe.wait_ge(slot_inT_ready, B + 1)
                for e in range(E):
                    ps = bank[2 + e // 8][0:H, (e % 8) * B * S:(e % 8 + 1) * B * S]
                    for kb in range(KB):
                        last = nc.tensor.matmul(ps, w1_sb[:, kb, e, :], slot_inT[:, kb, :, e * S:(e + 1) * S],
                                                start=(kb == 0), stop=(kb == KB - 1))
                    if e % 8 == 7:
                        last.then_inc(hs_done, 1)
                pe.wait_ge(w2_loaded, 16)
                for half in range(2):
                    pe.wait_ge(hs_ready, half + 1)
                    for db in range(KB):
                        ps = bank[(4, 0)[db] + half]
                        for e in range(8 * half, 8 * half + 8):
                            last = nc.tensor.matmul(ps[:, (e % 8) * B * S:(e % 8 + 1) * B * S],
                                                    w2_sb[:, e, db * P:(db + 1) * P], hs[:, e, :],
                                                    start=True, stop=True)
                        last.then_inc(soT_done, 1)
                pe.wait_ge(soT_ready, 4)
                for n in range(B):
                    for s in range(SB):
                        for db in range(KB):
                            at = s * D + db * P
                            last = nc.tensor.transpose(bank[(6, 7, 0, 1)[n]][:, at:at + P],
                                                       soT[:, db, n, s * P:(s + 1) * P], ident[:, :])
                    last.then_inc(so_done, 1)
                pe.wait_ge(so_ready, 4)
                with pe.Fori(0, B) as b:
                    for q in range(GB):
                        k = GB * b + q
                        pe.wait_ge(eT_staged, k + 1)
                        for t in range(GT):
                            pe.wait_ge(mix_scaled, GT * k + t + 1)
                            for s in range(SB):
                                last = nc.tensor.matmul(mix_ps[t][:, 0:D], eT[q % 2][:, s, t * P:(t + 1) * P],
                                                        so[:, bass.ds(b, 1), s, :], start=(s == 0),
                                                        stop=(s == SB - 1))
                            last.then_inc(mixed, 1)

            @block.vector
            def _(dve):
                def scale_tokens(k, q):
                    dve.wait_ge(tile_folded, GT * k + GT)
                    for t in range(GT):
                        tile = GT * k + t
                        nc.vector.scalar_tensor_tensor(
                            out=xn[q][:, t, 0:D], in0=x1_all[:, bass.ds(tile, 1), :].rearrange("p o d -> p (o d)"),
                            scalar=r2_all[:, bass.ds(tile, 1)], in1=g_rows[:, :],
                            op0=ALU.mult, op1=ALU.mult).then_inc(tok_scaled, 1)

                def floor_norms(k, q):
                    dve.wait_ge(n2_ready, GT * k + GT + 1)
                    nc.vector.tensor_scalar(n2_low[:, q, :], n2[:, q, :], NORM_EPS ** 2, None, ALU.max
                                            ).then_inc(n2_floored, 1)

                def split_xnT(k, q):
                    for kb in range(KB):
                        dve.wait_ge(xnT_rounded, KB * k + kb + 1)
                        nc.vector.tensor_tensor(xnT_lo[q % 2][:, kb, :], xnT_ps[kb][:, :],
                                                xnT_hi[q % 2][:, kb, :].bitcast(F32), ALU.subtract
                                                ).then_inc(xnT_split, 1)

                def copy_eT(b, t):
                    dve.wait_ge(eT_done, TB * b + t + 1)
                    nc.vector.tensor_copy(ET_all[:, :, bass.ds((TB * b + t) * P, P)],
                                          eT_ps[t % 2][:, 0:ES].rearrange("p (s n) -> p s n", s=SB)
                                          ).then_inc(eT_ready, 1)

                def route(b, last):
                    for t in range(TB):
                        q, k = t // GT, GB * b + t // GT
                        copy_eT(b, t)
                        if t == TB - 1:
                            normalise_slots(b)
                        if t % GT == 1 and not (last and q == GB - 1):
                            floor_norms(k + 1, (q + 1) % GB)
                        if t % GT == 2 and not (last and q >= GB - 3):
                            scale_tokens(k + 3, (q + 3) % GB)
                        if t % GT == 3 and not (last and q >= GB - 2):
                            split_xnT(k + 2, (q + 2) % GB)

                def normalise_slots(b):
                    dve.wait_ge(tile_folded, TB * b + 2 * TB)
                    for s in range(SB):
                        nc.vector.reciprocal(colinv[:, s:s + 1], fold_ps[s][:, D:D + 1]).then_inc(colinv_ready, 1)
                    for s in range(SB):
                        dve.wait_ge(colinv_ready, SB * b + s + 1)
                        nc.vector.tensor_scalar(slot_in[:, s, :], fold_ps[s][:, 0:D], colinv[:, s:s + 1], None,
                                                ALU.mult).then_inc(slot_in_ready, 1)
                    nc.vector.reciprocal(rinv[:, bass.ds(TB * b, TB)], rsum[:, bass.ds(TB * b, TB)]
                                         ).then_inc(rinv_ready, 1)

                scale_tokens(0, 0)
                scale_tokens(1, 1)
                scale_tokens(2, 2)
                floor_norms(0, 0)
                split_xnT(0, 0)
                split_xnT(1, 1)
                with dve.Fori(0, B - 1) as b:
                    route(b, last=False)
                route(B - 1, last=True)

                for half in range(2):
                    dve.wait_ge(hs_done, half + 1)
                    eh = slice(half * E // 2, (half + 1) * E // 2)
                    nc.vector.tensor_tensor(hs[:, eh, :],
                                            bank[2 + half][0:H, :].rearrange("p (e n) -> p e n", e=E // 2),
                                            b1T[0:H, eh].unsqueeze(2).to_broadcast([H, E // 2, B * S]),
                                            ALU.add).then_inc(hs_biased, 1)
                for half in range(2):
                    for db in range(KB):
                        dve.wait_ge(soT_done, KB * half + db + 1)
                        eh = slice(half * E // 2, (half + 1) * E // 2)
                        for n in range(B):
                            last = nc.vector.tensor_tensor(
                                soT[:, db, n, :].rearrange("p (e s) -> p e s", s=S)[:, eh, :],
                                bank[(4, 0)[db] + half][:, :].rearrange("p (e n s) -> p e n s", n=B, s=S)[:, :, n, :],
                                b2T[:, db, eh].unsqueeze(2).to_broadcast([P, E // 2, S]), ALU.add)
                        last.then_inc(soT_ready, 1)

                def y_statistics(k, q):
                    dve.wait_ge(y_ready, k + 1)
                    for t in range(GT):
                        nc.vector.bn_stats(st_y[:, t, :], y[q][:, t, 0:D])
                    dve.drain()
                    for t in range(GT):
                        nc.vector.bn_aggr(mv_y[:, q % 2, t, :], st_y[:, t, :]).then_inc(y_mv, 1)
                    dve.wait_ge(y_mv, GT * k + GT)
                    nc.vector.tensor_scalar(ve_y[:, q % 2, :], mv_y[:, q % 2, :, 1], LN_EPS, None,
                                            ALU.add).then_inc(y_ve, 1)

                def norm_y(k, q):
                    dve.wait_ge(y_rs, k + 1)
                    for t in range(GT):
                        nc.vector.tensor_scalar(y[q][:, t, 0:D], y[q][:, t, 0:D], mv_y[:, q % 2, t, 0:1],
                                                rs_y[:, q % 2, t:t + 1], ALU.subtract, ALU.mult).then_inc(y_normed, 1)

                def finish(b, last):
                    for q in range(GB):
                        if not (last and q == GB - 1):
                            y_statistics(GB * b + q + 1, (q + 1) % GB)
                        norm_y(GB * b + q, q)

                y_statistics(0, 0)
                with dve.Fori(0, B - 1) as b:
                    finish(b, last=False)
                finish(B - 1, last=True)
        return nc


_INS = ["x", "W1q", "b1q", "W2q", "b2q", "W1k", "b1k", "W2k", "b2k", "W1v", "b1v", "W2v", "b2v", "ln_w", "ln_b",
        "ln_gamma", "ln_beta", "mu", "scale", "w1", "b1", "w2", "b2"]
_NAMES = ["L0_attn_" + n for n in _INS[:15]] + ["L0_ffn_" + n for n in _INS[15:]]


def kernel(**inputs):
    import numpy as _np
    import concourse.bacc as _bacc
    from concourse import mybir as _mybir
    from concourse.bass_utils import run_bass_kernel_spmd as _run

    nc = _bacc.Bacc("TRN2", target_bir_lowering=False, num_devices=1)
    arrays, args = {}, []
    for name in _NAMES:
        a = _np.ascontiguousarray(inputs[name])
        arrays[f"in_{name}"] = a
        args.append(nc.dram_tensor(f"in_{name}", a.shape, _mybir.dt.from_np(a.dtype), kind="ExternalInput").ap())
    shape = inputs["L0_attn_x"].shape
    args.append(nc.dram_tensor("out_0", shape, _mybir.dt.from_np(_np.dtype("float32")), kind="ExternalOutput").ap())
    build(nc, *args)
    r = _run(nc, [arrays], core_ids=[0])
    return r.results[0]["out_0"]
```

```python
from contextlib import ExitStack

import concourse.bass as bass
from concourse import mybir

F32 = mybir.dt.float32
F32R = mybir.dt.float32r
ALU = mybir.AluOpType
ACT = mybir.ActivationFunctionType

P = 128
GT = 4
LN_EPS = 1e-5
NORM_EPS = 1e-12
BANK = 512


def build(nc, x, W1q, b1q, W2q, b2q, W1k, b1k, W2k, b2k, W1v, b1v, W2v, b2v, ln_w, ln_b,
          gamma, beta, mu, scale, w1, b1, w2, b2, out):
    B, T, D = x.shape
    _, E, S = mu.shape
    H = w1.shape[2]
    ES = E * S
    KB = D // P
    SB = ES // P
    TILES = B * T // P
    GROUPS = TILES // GT
    GB = GROUPS // B
    TB = TILES // B
    GTOK = GT * P
    assert D == 256 and ES == 256 and GTOK == BANK and KB == 2 and SB == 2 and H == 64
    SCORE_DIV2 = 256.0 * 512.0

    x_t = x.rearrange("b (t p) d -> p (b t) d", p=P)
    out_t = out.rearrange("b (t p) d -> p (b t) d", p=P)

    top = ExitStack()
    with top:
        def sb(name, shape, dt=F32, ctx=top):
            return ctx.enter_context(nc.sbuf_tensor(name, shape, dt))

        def sem(name, ctx=top):
            return ctx.enter_context(nc.semaphore(name))

        bank = [top.enter_context(nc.psum_tensor(f"bank{i}", [P, BANK], F32)) for i in range(8)]

        x1_all = sb("x1_all", [P, TILES, D])
        r2_all = sb("r2_all", [P, TILES])
        ident = sb("ident", [P, P])
        g_rows = sb("g_rows", [P, D])
        b_rows = sb("b_rows", [P, D])
        mu_hi = sb("mu_hi", [P, KB, ES], F32R)
        mu_lo = sb("mu_lo", [P, KB, ES], F32R)
        scale_col = sb("scale_col", [P, 1])
        shift = sb("shift", [P, 1])
        xn_all = sb("xn_all", [P, GB * GT * (D + 1)])
        xn = [xn_all[:, q * GT * (D + 1):(q + 1) * GT * (D + 1)].rearrange("p (t d) -> p t d", t=GT)
              for q in range(GB)]
        xnT_hi = [sb("xnT_hi0", [P, KB, GTOK], F32R)]
        xnT_lo = [sb("xnT_lo0", [P, KB, GTOK], F32R)]
        xnT_ps = bank[0:2]
        square = sb("square", [P, 2, D])
        n2 = sb("n2", [P, GB, GT])
        n2_low = sb("n2_low", [P, GB, GT])
        xinv = sb("xinv", [P, GB, GT])
        mv_z = sb("mv_z", [P, GT, 2])
        ve_z = sb("ve_z", [P, 2, GT])
        r_z = sb("r_z", [P, 2, GT])
        vinv = sb("vinv", [P, GT])
        var_x1 = sb("var_x1", [P, GT])
        minus_half = sb("minus_half", [P, 2, GT])
        z_mv = sem("z_mv")
        z_ve = sem("z_ve")
        z_vinv = sem("z_vinv")
        x1_var = sem("x1_var")
        x1_ve = sem("x1_ve")
        z_rs = sem("z_rs")
        x1_ready = sem("x1_ready")
        r2_ready = sem("r2_ready")
        tok_scaled = sem("tok_scaled")
        xn_ready = sem("xn_ready")
        n2_ready = sem("n2_ready")
        n2_floored = sem("n2_floored")
        xinv_ready = sem("xinv_ready")
        xnT_done = sem("xnT_done")
        xnT_rounded = sem("xnT_rounded")
        xnT_split = sem("xnT_split")
        b1T = sb("b1T", [P, E])
        b2T = sb("b2T", [P, KB, E])

        def norm_z(dve, a):
            var = mv_z[:, :, 1]
            dve.wait_ge(z_mv, GT * a + GT)
            nc.vector.tensor_scalar(ve_z[:, 0, :], var, LN_EPS, None, ALU.add).then_inc(z_ve, 1)
            dve.wait_ge(z_ve, a + 1)
            nc.vector.reciprocal(vinv[:, :], ve_z[:, 0, :]).then_inc(z_vinv, 1)
            dve.wait_ge(z_vinv, a + 1)
            nc.vector.tensor_tensor(var_x1[:, :], var, vinv[:, :], ALU.mult).then_inc(x1_var, 1)
            dve.wait_ge(x1_var, a + 1)
            nc.vector.tensor_scalar(ve_z[:, 1, :], var_x1[:, :], LN_EPS, None, ALU.add).then_inc(x1_ve, 1)

        def apply_z(dve, a):
            dve.wait_ge(z_rs, a + 1)
            for c in range(GT):
                xc = x1_all[:, bass.ds(GT * a + c, 1), :]
                nc.vector.tensor_scalar(xc, xc, mv_z[:, c, 0:1], r_z[:, 0, c:c + 1],
                                        ALU.subtract, ALU.mult).then_inc(x1_ready, 1)
            nc.vector.tensor_copy(r2_all[:, bass.ds(GT * a, GT)], r_z[:, 1, :]).then_inc(r2_ready, 1)

        def invert_z(pool, a):
            pool.wait_ge(x1_ve, a + 1)
            pool.tensor_tensor(r_z[:, :, :], ve_z[:, :, :], minus_half[:, :, :], ALU.pow).then_inc(z_rs, 1)

        def scale_tokens(k, q):
            for t in range(GT):
                tile = GT * k + t
                nc.vector.scalar_tensor_tensor(
                    out=xn[q][:, t, 0:D], in0=x1_all[:, bass.ds(tile, 1), :].rearrange("p o d -> p (o d)"),
                    scalar=r2_all[:, bass.ds(tile, 1)], in1=g_rows[:, :],
                    op0=ALU.mult, op1=ALU.mult).then_inc(tok_scaled, 1)

        def add_beta(engine, k, q):
            engine.wait_ge(tok_scaled, GT * k + GT)
            engine.tensor_tensor(xn[q][:, :, 0:D], xn[q][:, :, 0:D],
                               b_rows[:, :].unsqueeze(1).to_broadcast([P, GT, D]), ALU.add).then_inc(xn_ready, 1)

        def norms(act, k, q, tiles):
            act.wait_ge(xn_ready, k + 1)
            for t in tiles:
                act.wait_ge(n2_ready, GT * k + max(t - 1, 0) + 1)
                nc.scalar.activation(square[:, t % 2, :], xn[q][:, t, 0:D], ACT.Square,
                                     accum_out=n2[:, q, t:t + 1]).then_inc(n2_ready, 1)

        def floor_norms(dve, k, q):
            dve.wait_ge(n2_ready, GT * k + GT + 1)
            nc.vector.tensor_scalar(n2_low[:, q, :], n2[:, q, :], NORM_EPS ** 2, None, ALU.max
                                    ).then_inc(n2_floored, 1)

        def invert_norms(pool, k, q, exponent):
            pool.wait_ge(n2_floored, k + 1)
            pool.tensor_tensor(xinv[:, q, :], n2_low[:, q, :], exponent, ALU.pow).then_inc(xinv_ready, 1)

        def turn_xn(pe, k, q):
            pe.wait_ge(xn_ready, k + 1)
            if not (isinstance(k, int) and k == 0):
                pe.wait_ge(xnT_split, KB * k)
            for kb in range(KB):
                for t in range(GT):
                    last = nc.tensor.transpose(xnT_ps[kb][:, t * P:(t + 1) * P],
                                               xn[q][:, t, kb * P:(kb + 1) * P], ident[:, :])
            last.then_inc(xnT_done, 1)

        def round_xnT(act, k, q):
            act.wait_ge(xnT_done, k + 1)
            for kb in range(KB):
                nc.scalar.copy(xnT_hi[q % 2][:, kb, :], xnT_ps[kb][:, :]).then_inc(xnT_rounded, 1)

        def split_xnT(dve, k, q):
            for kb in range(KB):
                dve.wait_ge(xnT_rounded, KB * k + kb + 1)
                nc.vector.tensor_tensor(xnT_lo[q % 2][:, kb, :], xnT_ps[kb][:, :],
                                        xnT_hi[q % 2][:, kb, :].bitcast(F32), ALU.subtract).then_inc(xnT_split, 1)

        with ExitStack() as attn:
            def asb(name, shape, dt=F32):
                return sb(name, shape, dt, attn)

            def asem(name):
                return sem(name, attn)

            w_in = xn_all[:, 0:6 * KB * D].rearrange("p (a k n) -> p a k n", a=6, k=KB)
            kT = xn_all[:, 0:KB * GTOK].rearrange("p (k n) -> p k n", k=KB)
            v_tok = xn_all[:, GT * D:2 * GT * D].rearrange("p (t d) -> p t d", t=GT)
            at_att = 2 * GT * (D + 1)
            att = xn_all[:, at_att:at_att + GT * D].rearrange("p (t d) -> p t d", t=GT)
            at_x = at_att + GT * D
            x_in = xn_all[:, at_x:at_x + GT * D].rearrange("p (t d) -> p t d", t=GT)
            w_hi = asb("w_hi", [P, 6, KB, D], F32R)
            w_lo = asb("w_lo", [P, 6, KB, D], F32R)
            bias_rows = asb("bias_rows", [5 * KB, P])
            bias_col = asb("bias_col", [P, 5 * KB])
            b2v_rows = asb("b2v_rows", [P, D])
            lnw_rows = asb("lnw_rows", [P, D])
            lnb_rows = asb("lnb_rows", [P, D])
            causal = asb("causal", [P, GT, P])
            keep = asb("keep", [P, GROUPS])
            xT_hi, xT_lo = xnT_hi[0], xnT_lo[0]
            h = asb("h", [P, 2, GTOK])
            zeros = h[:, 0, :]
            h_hi = asb("h_hi", [P, 3, KB, GTOK], F32R)
            h_lo = asb("h_lo", [P, 3, KB, GTOK], F32R)
            q_hi = asb("q_hi", [P, KB, GTOK], F32R)
            q_lo = asb("q_lo", [P, KB, GTOK], F32R)
            k_hi = asb("k_hi", [P, KB, GTOK], F32R)
            k_lo = asb("k_lo", [P, KB, GTOK], F32R)
            v_hi = asb("v_hi", [P, GT, D], F32R)
            v_lo = asb("v_lo", [P, GT, D], F32R)
            ktok_hi = asb("ktok_hi", [P, GT, D], F32R)
            ktok_lo = asb("ktok_lo", [P, GT, D], F32R)
            masked = asb("masked", [P, GT, P])
            masked_hi = asb("masked_hi", [P, GT, P], F32R)
            masked_lo = asb("masked_lo", [P, GT, P], F32R)
            state_hi = asb("state_hi", [P, KB, D], F32R)
            state_lo = asb("state_lo", [P, KB, D], F32R)
            st_o = asb("st_o", [P, GT, 6])
            mv_o = asb("mv_o", [P, GT, 2])
            rs_o = asb("rs_o", [P, GT])
            st_z = asb("st_z", [P, GT, 6])
            ve_o = asb("ve_o", [P, GT])
            warm = asb("warm", [P, GT])

            mu_in = asb("mu_in", [P, KB, ES])
            mu_unit = asb("mu_unit", [P, KB, ES])
            mu_sq = mu_unit
            mu_n2 = asb("mu_n2", [P, SB])
            mu_inv = asb("mu_inv", [P, SB])
            mu_fac = asb("mu_fac", [P, SB])
            mu_diag = asb("mu_diag", [P, SB, P])
            ones = asb("ones", [P, P])
            b1_row = asb("b1_row", [E, P])
            b2_row = asb("b2_row", [E, D])

            moe_loaded = asem("moe_loaded")
            b1_blank = asem("b1_blank")
            mu_squared = asem("mu_squared")
            mu_summed = asem("mu_summed")
            mu_floored = asem("mu_floored")
            mu_rs = asem("mu_rs")
            mu_scaled = asem("mu_scaled")
            mu_spread = asem("mu_spread")
            mu_rows = asem("mu_rows")
            mu_united = asem("mu_united")
            mu_rounded = asem("mu_rounded")
            mu_ready = asem("mu_ready")
            scale_neg = asem("scale_neg")
            shift_ready = asem("shift_ready")
            moe_turned = asem("moe_turned")
            moe_ready = asem("moe_ready")
            x_loaded = asem("x_loaded")
            weight_loaded = [asem(f"weight_loaded{n}") for n in range(6)]
            bias_loaded = asem("bias_loaded")
            rows_loaded = asem("rows_loaded")
            table_warm = asem("table_warm")
            ident_blank = asem("ident_blank")
            masks_ready = asem("masks_ready")
            keep_blank = asem("keep_blank")
            keep_ready = asem("keep_ready")
            w_rounded = asem("w_rounded")
            w_split = asem("w_split")
            bias_turned = asem("bias_turned")
            bias_ready = asem("bias_ready")
            xT_done = asem("xT_done")
            x_rounded = asem("x_rounded")
            x_split = asem("x_split")
            hidden_done = asem("hidden_done")
            h_rounded = asem("h_rounded")
            hqk_split = asem("hqk_split")
            hv_split = asem("hv_split")
            qk_done = asem("qk_done")
            q_rounded = asem("q_rounded")
            q_split = asem("q_split")
            k_rounded = asem("k_rounded")
            k_split = asem("k_split")
            v_done = asem("v_done")
            v_biased = asem("v_biased")
            v_rounded = asem("v_rounded")
            v_split0 = asem("v_split0")
            v_split1 = asem("v_split1")
            kt_done = asem("kt_done")
            ktok_rounded = asem("ktok_rounded")
            ktok_split = asem("ktok_split")
            scores_done = asem("scores_done")
            scores_masked = asem("scores_masked")
            masked_rounded = asem("masked_rounded")
            masked_split = asem("masked_split")
            state_updated = asem("state_updated")
            state_gated = asem("state_gated")
            state_rounded = asem("state_rounded")
            state_split = asem("state_split")
            chunk_done = asem("chunk_done")
            chunk_mv = asem("chunk_mv")
            chunk_ve = asem("chunk_ve")
            chunk_rs = asem("chunk_rs")
            chunk_normed = asem("chunk_normed")
            xb_ready = asem("xb_ready")
            att_weighted = asem("att_weighted")
            z_ready = asem("z_ready")

            XT0, XT1, Q1, K1, V1, Q2, K2, V2, KT = 0, 1, 2, 4, 6, 8, 10, 12, 14
            scores_ps, state_ps, chunk_ps = bank[4], bank[5], [bank[6], bank[7]]
            LAYERS = {"q": 0, "k": 1, "v": 2}

            tail_ps = [bank[6], bank[7], bank[2], bank[3]]
            tail_hi = [state_hi, h_hi[:, 0, :, 0:D]]
            tail_lo = [state_lo, h_lo[:, 0, :, 0:D]]

            def job_bank(job):
                return bank[job % 4]

            def run_groups(body, engine, after_first, before_last):
                body(0, attend=False)
                after_first()
                with engine.Fori(1, GROUPS) as g:
                    body(g, attend=True)
                before_last()
                body(GROUPS, attend=True, project=False)

            block = attn.enter_context(nc.Block())

            @block.sync
            def _(sp):
                def load_x(g):
                    sp.dma_start(x_in[:, :, :], x_t[:, bass.ds(g * GT, GT), :]).then_inc(x_loaded, 16)

                load_x(0)
                for n, w in enumerate((W1q, W1k, W1v, W2q, W2k, W2v)):
                    sp.dma_start(w_in[:, n, :, :], w.rearrange("(k p) n -> p k n", p=P)).then_inc(weight_loaded[n], 16)
                for src, tile in ((b2v, b2v_rows), (ln_b, lnb_rows), (ln_w, lnw_rows)):
                    sp.dma_start(tile[:, :], src.partition_broadcast(P)).then_inc(rows_loaded, 16)
                for src, tile in ((gamma, g_rows), (beta, b_rows), (scale, scale_col)):
                    sp.dma_start(tile[:, :], src.partition_broadcast(P)).then_inc(moe_loaded, 16)
                sp.dma_start(mu_in[:, :, :], mu.rearrange("(k p) e s -> p k (e s)", p=P)).then_inc(moe_loaded, 16)
                sp.dma_start(b2_row[:, :], b2).then_inc(moe_loaded, 16)
                sp.wait_ge(b1_blank, 1)
                sp.dma_start(b1_row[:, 0:H], b1).then_inc(moe_loaded, 16)
                with sp.Fori(1, GROUPS) as g:
                    sp.wait_ge(xT_done, 2 * g)
                    sp.wait_ge(xb_ready, g)
                    load_x(g)

            @block.gpsimd
            def _(pool):
                pool.memset(ident[:, :], 0.0)
                pool.memset(causal[:, :, :], 1.0)
                pool.memset(keep[:, :], 1.0)
                pool.memset(minus_half[:, :, :], -0.5)
                pool.memset(ones[:, :], 1.0)
                pool.memset(n2[:, :, :], 0.0).then_inc(n2_ready, 1)
                pool.memset(b1_row[:, :], 0.0).then_inc(b1_blank, 1)
                pool.memset(zeros, 0.0).then_inc(ident_blank, 1)
                pool.wait_ge(ident_blank, 1)
                pool.affine_select(out=ident[:, :], in_=ident[:, :], compare_op=ALU.not_equal, fill=1.0,
                                   base=0, pattern=[[-1, P]], channel_multiplier=1)
                pool.affine_select(out=causal[:, :, :], in_=causal[:, :, :], compare_op=ALU.is_ge, fill=0.0,
                                   base=0, pattern=[[0, GT], [1, P]], channel_multiplier=-1)
                pool.memset(keep[:, :].rearrange("p (b g) -> p b g", g=GB)[:, :, 0:1], 0.0).then_inc(masks_ready, 1)

                def split_hv(g):
                    for m in range(2):
                        pool.wait_ge(h_rounded, 6 * g + 4 + m + 1)
                        pool.tensor_tensor(h_lo[:, 2, m, :], h[:, m, :], h_hi[:, 2, m, :].bitcast(F32),
                                           ALU.subtract).then_inc(hv_split, 1)

                def add_ln_b(g):
                    pool.wait_ge(x_loaded, 16 * (g + 1))
                    if isinstance(g, int) and g == 0:
                        pool.wait_ge(rows_loaded, 16 * 3)
                    pool.tensor_tensor(x1_all[:, bass.ds(g * GT, GT), :], x_in[:, :, :],
                                       lnb_rows[:, :].unsqueeze(1).to_broadcast([P, GT, D]),
                                       ALU.add).then_inc(xb_ready, 1)

                def body(g, attend, project=True):
                    if attend:
                        a = g - 1
                        for c in range(GT):
                            n = GT * a + c
                            pool.wait_ge(chunk_ve, n + 1)
                            pool.tensor_tensor(rs_o[:, c:c + 1], ve_o[:, c:c + 1], minus_half[:, 0, 0:1],
                                               ALU.pow).then_inc(chunk_rs, 1)
                            if project and c == 0:
                                add_ln_b(g)
                            pool.wait_ge(chunk_normed, n + 1 + 2)
                            pool.tensor_tensor(att[:, c, :], att[:, c, :], lnw_rows[:, :],
                                               ALU.mult).then_inc(att_weighted, 1)
                            pool.wait_ge(att_weighted, n + 1)
                            z = x1_all[:, bass.ds(n, 1), :]
                            pool.tensor_tensor(z, z, att[:, c:c + 1, :], ALU.add).then_inc(z_ready, 1)
                            if project and c == 2:
                                split_hv(g)
                    else:
                        add_ln_b(g)
                        split_hv(g)
                    if project:
                        split_v(g, 1)
                    if attend and project:
                        invert_z(pool, a)
                    if not project:
                        invert_norms(pool, 0, 0, minus_half[:, 0, :])

                def split_v(g, m):
                    pool.wait_ge(v_rounded, 2 * g + m + 1)
                    pair = slice(2 * m, 2 * m + 2)
                    pool.tensor_tensor(v_lo[:, pair, :], v_tok[:, pair, :], v_hi[:, pair, :].bitcast(F32),
                                       ALU.subtract).then_inc(v_split1, 1)

                def invert_mu_norms():
                    pool.wait_ge(mu_floored, 1)
                    pool.tensor_tensor(mu_inv[:, :], mu_n2[:, :], minus_half[:, 0, 0:SB], ALU.pow).then_inc(mu_rs, 1)

                run_groups(body, pool, invert_mu_norms, lambda: None)

            @block.scalar
            def _(act):
                rows = ((b1q, 0), (b1k, 1), (b1v, 2), (b2q, 3), (b2k, 4))
                for b_row, n in rows:
                    act.dma_start(bias_rows[KB * n:KB * n + KB, :],
                                  b_row.rearrange("(k p) -> k p", p=P)).then_inc(bias_loaded, 16)

                def round_state(a, c, to=state_hi):
                    act.wait_ge(state_updated, GT * a + c + 1)
                    if c == 0:
                        act.wait_ge(state_gated, a + 1)
                    nc.scalar.copy(to[:, :, :], state_ps[:, :].rearrange("p (k d) -> p k d", k=KB)
                                   ).then_inc(state_rounded, 1)

                def round_x(g, kb):
                    act.wait_ge(xT_done, 2 * g + kb + 1)
                    nc.scalar.copy(xT_hi[:, kb, :], job_bank(XT0 + kb)[:, :]).then_inc(x_rounded, 1)

                def hidden(g, n, m):
                    act.wait_ge(hidden_done, 6 * g + 2 * n + m + 1)
                    if n > 0:
                        act.wait_ge(hqk_split, 4 * g + 2 * (n - 1) + m + 1)
                    elif not (isinstance(g, int) and g == 0):
                        act.wait_ge(hv_split, 2 * g - 1 + m)
                    ps = job_bank(Q1 + 2 * n + m)
                    bias = bias_col[:, KB * n + m:KB * n + m + 1]
                    nc.scalar.activation(h[:, m, :], ps[:, :], ACT.Gelu, bias=bias)
                    nc.scalar.activation(h_hi[:, n, m, :], ps[:, :], ACT.Gelu, bias=bias).then_inc(h_rounded, 1)

                def round_q(g, m):
                    act.wait_ge(qk_done, 4 * g + m + 1)
                    nc.scalar.activation(q_hi[:, m, :], job_bank(Q2 + m)[:, :], ACT.Identity,
                                         bias=bias_col[:, KB * 3 + m:KB * 3 + m + 1]).then_inc(q_rounded, 1)

                def round_k(g, m):
                    act.wait_ge(qk_done, 4 * g + 2 + m + 1)
                    ps = job_bank(K2 + m)
                    bias = bias_col[:, KB * 4 + m:KB * 4 + m + 1]
                    nc.scalar.activation(kT[:, m, :], ps[:, :], ACT.Identity, bias=bias)
                    nc.scalar.activation(k_hi[:, m, :], ps[:, :], ACT.Identity, bias=bias).then_inc(k_rounded, 1)

                def round_v(g, m):
                    act.wait_ge(v_biased, 2 * g + m + 1)
                    pair = slice(2 * m, 2 * m + 2)
                    nc.scalar.copy(v_hi[:, pair, :], v_tok[:, pair, :]).then_inc(v_rounded, 1)

                def round_masked(g):
                    act.wait_ge(scores_masked, g + 1)
                    nc.scalar.copy(masked_hi[:, :, :], masked[:, :, :]).then_inc(masked_rounded, 1)

                def round_ktok(g, m):
                    act.wait_ge(kt_done, 2 * g + m + 1)
                    nc.scalar.copy(ktok_hi[:, 2 * m:2 * m + 2, :],
                                   job_bank(KT + m)[:, :].rearrange("p (t d) -> p t d", t=2)
                                   ).then_inc(ktok_rounded, 1)

                def square_mu():
                    act.wait_ge(moe_loaded, 16 * 6)
                    nc.scalar.activation(mu_sq[:, :, :], mu_in[:, :, :], ACT.Square).then_inc(mu_squared, 1)

                def body(g, attend, project=True):
                    a = g - 1
                    if project:
                        round_x(g, 0)
                        round_x(g, 1)
                    if not attend:
                        act.wait_ge(bias_turned, 1)
                        nc.scalar.copy(bias_col[:, :], bank[7][:, 0:5 * KB]).then_inc(bias_ready, 1)
                        act.wait_ge(bias_ready, 1)
                    for c in range(GT):
                        if attend and c + 1 < GT:
                            round_state(a, c + 1, state_hi if project else tail_hi[(c + 1) % 2])
                        if not project and c == GT - 2:
                            norms(act, 0, 0, range(GT))
                        if project and c < 3:
                            hidden(g, c, 0)
                            hidden(g, c, 1)
                    if not attend:
                        square_mu()
                    if project:
                        round_state(g, 0)
                        for m in range(KB):
                            round_q(g, m)
                        for m in range(KB):
                            round_k(g, m)
                        for m in range(2):
                            round_v(g, m)
                        round_masked(g)
                        for m in range(2):
                            round_ktok(g, m)

                act.wait_ge(z_ready, 1)
                nc.scalar.activation(warm[:, :], vinv[:, :], ACT.Gelu).then_inc(table_warm, 1)

                def copy_moe_biases():
                    act.wait_ge(moe_turned, 1)
                    nc.scalar.copy(b1T[:, :], bank[0][:, 0:E]).then_inc(moe_ready, 1)
                    nc.scalar.copy(b2T[:, :, :], bank[0][:, E:3 * E].rearrange("p (k e) -> p k e", k=KB)
                                   ).then_inc(moe_ready, 1)

                run_groups(body, act, lambda: None, copy_moe_biases)
                round_xnT(act, 0, 0)
                act.wait_ge(moe_ready, 2)
                act.wait_ge(table_warm, 1)

            @block.tensor
            def _(pe):
                def split3(ps, w, xs, start, stop):
                    nc.tensor.matmul(ps, w[0], xs[0], start=start, stop=False)
                    nc.tensor.matmul(ps, w[0], xs[1], start=False, stop=False)
                    return nc.tensor.matmul(ps, w[1], xs[0], start=False, stop=stop)

                def turn_x(g, kb):
                    if kb == 0:
                        pe.wait_ge(x_loaded, 16 * (g + 1))
                    if not (isinstance(g, int) and g == 0):
                        pe.wait_ge(v_biased, 2 * g - 1 + kb)
                    for t in range(GT):
                        last = nc.tensor.transpose(job_bank(XT0 + kb)[:, t * P:(t + 1) * P],
                                                   x_in[:, t, kb * P:(kb + 1) * P], ident[:, :])
                    last.then_inc(xT_done, 1)

                def hidden(g, n, m):
                    if n == 0:
                        if m == 0:
                            pe.wait_ge(x_split, 2 * g + 2)
                        if not (isinstance(g, int) and g == 0):
                            pe.wait_ge(ktok_split, 2 * g - 1 + m)
                    if n == 2:
                        pe.wait_ge(h_rounded, 6 * g + m + 1)
                    if isinstance(g, int) and g == 0:
                        pe.wait_ge(w_split, n + 1)
                    for kb in range(KB):
                        cols = slice(m * P, (m + 1) * P)
                        last = split3(job_bank(Q1 + 2 * n + m)[:, :],
                                      (w_hi[:, n, kb, cols], w_lo[:, n, kb, cols]),
                                      (xT_hi[:, kb, :], xT_lo[:, kb, :]), kb == 0, kb == KB - 1)
                    last.then_inc(hidden_done, 1)

                def project_qk(g, n, m):
                    pe.wait_ge(hqk_split, 4 * g + 2 * n + 2)
                    pe.wait_ge(h_rounded, 6 * g + 2 * (n + 1) + m + 1)
                    if isinstance(g, int) and g == 0:
                        pe.wait_ge(w_split, 3 + n + 1)
                    for kb in range(KB):
                        cols = slice(m * P, (m + 1) * P)
                        last = split3(job_bank(Q2 + 2 * n + m)[:, :],
                                      (w_hi[:, 3 + n, kb, cols], w_lo[:, 3 + n, kb, cols]),
                                      (h_hi[:, n, kb, :], h_lo[:, n, kb, :]), kb == 0, kb == KB - 1)
                    last.then_inc(qk_done, 1)

                def project_v(g, m):
                    pe.wait_ge(hv_split, 2 * g + 2)
                    pe.wait_ge(q_split, 2 * g + m + 1)
                    if isinstance(g, int) and g == 0:
                        pe.wait_ge(w_split, 6)
                    for half in range(2):
                        toks = slice((2 * m + half) * P, (2 * m + half + 1) * P)
                        for kb in range(KB):
                            last = split3(job_bank(V2 + m)[:, half * D:(half + 1) * D],
                                          (h_hi[:, 2, kb, toks], h_lo[:, 2, kb, toks]),
                                          (w_hi[:, 5, kb, :], w_lo[:, 5, kb, :]), kb == 0, kb == KB - 1)
                    last.then_inc(v_done, 1)

                def turn_k(g, m):
                    pe.wait_ge(k_rounded, 2 * g + 2)
                    for half in range(2):
                        for kb in range(KB):
                            at = half * D + kb * P
                            last = nc.tensor.transpose(
                                job_bank(KT + m)[:, at:at + P],
                                kT[:, kb, (2 * m + half) * P:(2 * m + half + 1) * P], ident[:, :])
                    last.then_inc(kt_done, 1)

                def scores(g):
                    if not (isinstance(g, int) and g == 0):
                        pe.wait_ge(scores_masked, g)
                    pe.wait_ge(q_split, 2 * g + 2)
                    pe.wait_ge(k_split, 2 * g + 2)
                    for c in range(GT):
                        toks = slice(c * P, (c + 1) * P)
                        for kb in range(KB):
                            last = split3(scores_ps[:, toks], (k_hi[:, kb, toks], k_lo[:, kb, toks]),
                                          (q_hi[:, kb, toks], q_lo[:, kb, toks]), kb == 0, kb == KB - 1)
                    last.then_inc(scores_done, 1)

                def chunk(a, c):
                    toks = slice(c * P, (c + 1) * P)
                    ps = chunk_ps[c % 2][:, 0:D]
                    pe.wait_ge(chunk_normed, GT * a + c + 1)
                    pe.wait_ge(state_split, GT * a + c + 1)
                    for kb in range(KB):
                        split3(ps, (q_hi[:, kb, toks], q_lo[:, kb, toks]),
                               (state_hi[:, kb, :], state_lo[:, kb, :]), kb == 0, False)
                    if c == 0:
                        pe.wait_ge(masked_split, a + 1)
                        pe.wait_ge(v_split0, a + 1)
                    if c == 2:
                        pe.wait_ge(v_split1, a + 1)
                    v = (v_hi[:, c, :], v_lo[:, c, :])
                    split3(ps, (masked_hi[:, c, :], masked_lo[:, c, :]), v, False, True).then_inc(chunk_done, 1)
                    if c % 2 == 0:
                        pe.wait_ge(ktok_split, 2 * a + c // 2 + 1)
                    update_state(c)

                def update_state(c):
                    for kb in range(KB):
                        state = state_ps[:, kb * D:(kb + 1) * D]
                        for w, r in ((ktok_hi, v_hi), (ktok_hi, v_lo), (ktok_lo, v_hi)):
                            last = nc.tensor.matmul(state, w[:, c, kb * P:(kb + 1) * P], r[:, c, :], start=False,
                                                    stop=False, skip_group_check=True)
                    last.then_inc(state_updated, 1)

                def last_chunks(a):
                    pe.wait_ge(masked_split, a + 1)
                    pe.wait_ge(v_split0, a + 1)
                    pe.wait_ge(v_split1, a + 1)
                    for c in range(GT):
                        if c < 2:
                            pe.wait_ge(chunk_normed, GT * a + c + 1)
                        else:
                            pe.wait_ge(ktok_split, 2 * a + 2)
                        split3(tail_ps[c][:, 0:D], (masked_hi[:, c, :], masked_lo[:, c, :]),
                               (v_hi[:, c, :], v_lo[:, c, :]), True, False)
                    for c in range(GT):
                        toks = slice(c * P, (c + 1) * P)
                        pe.wait_ge(state_split, GT * a + c + 1)
                        if c < GT - 1:
                            update_state(c)
                        for kb in range(KB):
                            last = split3(tail_ps[c][:, 0:D], (q_hi[:, kb, toks], q_lo[:, kb, toks]),
                                          (tail_hi[c % 2][:, kb, :], tail_lo[c % 2][:, kb, :]), False, kb == KB - 1)
                        last.then_inc(chunk_done, 1)

                def turn_biases():
                    pe.wait_ge(bias_loaded, 16 * 5)
                    nc.tensor.transpose(bank[7][:, 0:5 * KB], bias_rows[:, :], ident[0:5 * KB, 0:5 * KB]
                                        ).then_inc(bias_turned, 1)
                    nc.tensor.matmul(state_ps[:, :], ident[:, :], zeros, start=True, stop=True
                                     ).then_inc(state_updated, 1)
                    pe.wait_ge(bias_ready, 1)

                def sum_mu_squares():
                    pe.wait_ge(mu_squared, 1)
                    for sblk in range(SB):
                        for kb in range(KB):
                            last = nc.tensor.matmul(bank[7][:, sblk:sblk + 1], mu_sq[:, kb, sblk * P:(sblk + 1) * P],
                                                    ones[:, 0:1], start=(kb == 0), stop=(kb == KB - 1))
                    last.then_inc(mu_summed, 1)

                def body(g, attend, project=True):
                    a = g - 1
                    if project:
                        turn_x(g, 0)
                        turn_x(g, 1)
                    if not attend:
                        turn_biases()
                    if not project:
                        last_chunks(a)
                    for c in range(GT):
                        if attend and project:
                            chunk(a, c)
                        if project and c < 3:
                            hidden(g, c, 0)
                            hidden(g, c, 1)
                    if project:
                        for n in range(2):
                            project_qk(g, n, 0)
                            project_qk(g, n, 1)
                        project_v(g, 0)
                        project_v(g, 1)
                        if not attend:
                            sum_mu_squares()
                        scores(g)
                        turn_k(g, 0)
                        turn_k(g, 1)

                def turn_moe_rows():
                    pe.wait_ge(moe_loaded, 16 * 6)
                    pe.wait_ge(v_biased, 2 * GROUPS)
                    nc.tensor.transpose(bank[0][:, 0:E], b1_row[:, :], ident[0:E, 0:E])
                    for kb in range(KB):
                        last = nc.tensor.transpose(bank[0][:, (1 + kb) * E:(2 + kb) * E],
                                                   b2_row[:, kb * P:(kb + 1) * P], ident[0:E, 0:E])
                    last.then_inc(moe_turned, 1)
                    pe.wait_ge(mu_spread, SB)
                    for sblk in range(SB):
                        last = nc.tensor.matmul(bank[1][:, sblk * P:(sblk + 1) * P], ones[:, :], mu_diag[:, sblk, :],
                                                start=True, stop=True)
                    last.then_inc(mu_rows, 1)

                pe.wait_ge(masks_ready, 1)
                run_groups(body, pe, lambda: pe.wait_ge(mu_floored, 1),
                           turn_moe_rows)
                pe.wait_ge(moe_ready, 2)
                pe.wait_ge(mu_united, 1)
                turn_xn(pe, 0, 0)

            @block.vector
            def _(dve):
                nc.vector.memset(rs_o[:, :], 0.0).then_inc(chunk_normed, 2)
                nc.vector.memset(vinv[:, :], 0.0).then_inc(z_ready, 1)

                def split_weight(n):
                    dve.wait_ge(weight_loaded[n], 16)
                    nc.vector.tensor_copy(w_hi[:, n, :, :], w_in[:, n, :, :]).then_inc(w_rounded, 1)
                    dve.wait_ge(w_rounded, n + 1)
                    nc.vector.tensor_tensor(w_lo[:, n, :, :], w_in[:, n, :, :], w_hi[:, n, :, :].bitcast(F32),
                                            ALU.subtract).then_inc(w_split, 1)

                def gate_state(a):
                    dve.wait_ge(state_updated, GT * a + 1)
                    nc.vector.tensor_scalar(state_ps[:, :], state_ps[:, :], keep[:, bass.ds(a, 1)], None,
                                            ALU.mult).then_inc(state_gated, 1)

                def mask_scores(a):
                    dve.wait_ge(scores_done, a + 1)
                    nc.vector.tensor_tensor(masked[:, :, :], scores_ps[:, :].rearrange("p (c n) -> p c n", c=GT),
                                            causal[:, :, :], ALU.mult).then_inc(scores_masked, 1)

                def split_x(g, kb):
                    dve.wait_ge(x_rounded, 2 * g + kb + 1)
                    nc.vector.tensor_tensor(xT_lo[:, kb, :], job_bank(XT0 + kb)[:, :],
                                            xT_hi[:, kb, :].bitcast(F32), ALU.subtract).then_inc(x_split, 1)

                def split_state(a, c, hi=state_hi, lo=state_lo):
                    dve.wait_ge(state_rounded, GT * a + c + 1)
                    nc.vector.tensor_tensor(lo[:, :, :], state_ps[:, :].rearrange("p (k d) -> p k d", k=KB),
                                            hi[:, :, :].bitcast(F32), ALU.subtract).then_inc(state_split, 1)

                def split_masked(g):
                    dve.wait_ge(masked_rounded, g + 1)
                    nc.vector.tensor_tensor(masked_lo[:, :, :], masked[:, :, :], masked_hi[:, :, :].bitcast(F32),
                                            ALU.subtract).then_inc(masked_split, 1)

                def split_q(g, m):
                    dve.wait_ge(q_rounded, 2 * g + m + 1)
                    nc.vector.scalar_tensor_tensor(
                        out=q_lo[:, m, :], in0=job_bank(Q2 + m)[:, :], scalar=bias_col[:, KB * 3 + m:KB * 3 + m + 1],
                        in1=q_hi[:, m, :].bitcast(F32), op0=ALU.add, op1=ALU.subtract).then_inc(q_split, 1)

                def split_k(g, m):
                    dve.wait_ge(k_rounded, 2 * g + m + 1)
                    nc.vector.tensor_tensor(k_lo[:, m, :], kT[:, m, :], k_hi[:, m, :].bitcast(F32),
                                            ALU.subtract).then_inc(k_split, 1)

                def split_ktok(g, m):
                    dve.wait_ge(ktok_rounded, 2 * g + m + 1)
                    pair = slice(2 * m, 2 * m + 2)
                    nc.vector.tensor_tensor(ktok_lo[:, pair, :],
                                            job_bank(KT + m)[:, :].rearrange("p (t d) -> p t d", t=2),
                                            ktok_hi[:, pair, :].bitcast(F32), ALU.subtract).then_inc(ktok_split, 1)

                def split_h(g, n, m):
                    dve.wait_ge(h_rounded, 6 * g + 2 * n + m + 1)
                    nc.vector.tensor_tensor(h_lo[:, n, m, :], h[:, m, :], h_hi[:, n, m, :].bitcast(F32),
                                            ALU.subtract).then_inc(hqk_split, 1)

                def bias_v(g, m):
                    dve.wait_ge(v_done, 2 * g + m + 1)
                    nc.vector.tensor_tensor(v_tok[:, 2 * m:2 * m + 2, :],
                                            job_bank(V2 + m)[:, :].rearrange("p (t d) -> p t d", t=2),
                                            b2v_rows[:, :].unsqueeze(1).to_broadcast([P, 2, D]),
                                            ALU.add).then_inc(v_biased, 1)

                def split_v(g, m):
                    dve.wait_ge(v_rounded, 2 * g + m + 1)
                    pair = slice(2 * m, 2 * m + 2)
                    nc.vector.tensor_tensor(v_lo[:, pair, :], v_tok[:, pair, :], v_hi[:, pair, :].bitcast(F32),
                                            ALU.subtract).then_inc(v_split0, 1)

                def chunk_statistics(a, c, ps):
                    n = GT * a + c
                    dve.wait_ge(chunk_done, n + 1)
                    nc.vector.bn_stats(st_o[:, c, :], ps[:, 0:D])
                    dve.drain()
                    nc.vector.bn_aggr(mv_o[:, c, :], st_o[:, c, :]).then_inc(chunk_mv, 1)
                    dve.wait_ge(chunk_mv, n + 1)
                    nc.vector.tensor_scalar(ve_o[:, c:c + 1], mv_o[:, c, 1:2], LN_EPS * SCORE_DIV2, None,
                                            ALU.add).then_inc(chunk_ve, 1)

                def norm_chunk(a, c, ps):
                    n = GT * a + c
                    dve.wait_ge(chunk_rs, n + 1)
                    if c == 0:
                        dve.wait_ge(z_ready, GT * a + 1)
                    nc.vector.tensor_scalar(att[:, c, :], ps[:, 0:D], mv_o[:, c, 0:1],
                                            rs_o[:, c:c + 1], ALU.subtract, ALU.mult).then_inc(chunk_normed, 1)

                def z_statistics(a, c):
                    n = GT * a + c
                    dve.wait_ge(z_ready, n + 2)
                    nc.vector.bn_stats(st_z[:, c, :], x1_all[:, bass.ds(n, 1), :])
                    dve.drain()
                    nc.vector.bn_aggr(mv_z[:, c, :], st_z[:, c, :]).then_inc(z_mv, 1)

                def floor_mu():
                    dve.wait_ge(mu_summed, 1)
                    nc.vector.tensor_scalar(mu_n2[:, :], bank[7][:, 0:SB], NORM_EPS ** 2, None, ALU.max
                                            ).then_inc(mu_floored, 1)

                def mu_factors():
                    nc.vector.tensor_scalar(shift[:, :], scale_col[:, :], -1.0, None, ALU.mult).then_inc(scale_neg, 1)
                    dve.wait_ge(scale_neg, 1)
                    nc.vector.tensor_tensor(shift[:, :], shift[:, :], scale_col[:, :], ALU.min).then_inc(shift_ready, 1)
                    dve.wait_ge(mu_rs, 1)
                    nc.vector.tensor_scalar(mu_fac[:, :], mu_inv[:, :], scale_col[:, :], None,
                                            ALU.mult).then_inc(mu_scaled, 1)
                    dve.wait_ge(mu_scaled, 1)
                    for sblk in range(SB):
                        nc.vector.tensor_scalar(mu_diag[:, sblk, :], ident[:, :], mu_fac[:, sblk:sblk + 1], None,
                                                ALU.mult).then_inc(mu_spread, 1)

                def mu_units():
                    dve.wait_ge(mu_rows, 1)
                    nc.vector.tensor_tensor(mu_unit[:, :, :], mu_in[:, :, :],
                                            bank[1][:, 0:ES].unsqueeze(1).to_broadcast([P, KB, ES]),
                                            ALU.mult).then_inc(mu_united, 1)
                    dve.wait_ge(mu_united, 1)
                    nc.vector.tensor_copy(mu_hi[:, :, :], mu_unit[:, :, :]).then_inc(mu_rounded, 1)
                    dve.wait_ge(mu_rounded, 1)
                    nc.vector.tensor_tensor(mu_lo[:, :, :], mu_unit[:, :, :], mu_hi[:, :, :].bitcast(F32),
                                            ALU.subtract).then_inc(mu_ready, 1)

                def body(g, attend, project=True, more=True):
                    a = g - 1
                    for c in range(GT):
                        if attend and c + 1 < GT:
                            if project:
                                split_state(a, c + 1)
                            else:
                                split_state(a, c + 1, tail_hi[(c + 1) % 2], tail_lo[(c + 1) % 2])
                        if attend and c > 1:
                            z_statistics(a, c - 2)
                        if attend:
                            ps = chunk_ps[c % 2] if project else tail_ps[c]
                            chunk_statistics(a, c, ps)
                        if project and c < 2:
                            split_h(g, c, 0)
                            split_h(g, c, 1)
                        if not project:
                            (mu_units, lambda: scale_tokens(0, 0), lambda: add_beta(dve, 0, 0),
                             lambda: scale_tokens(1, 1))[c]()
                        if attend and c < GT - 1:
                            norm_chunk(a, c, ps)
                    if project:
                        gate_state(g)
                        split_state(g, 0)
                        split_q(g, 0)
                        split_q(g, 1)
                    if attend:
                        norm_chunk(a, GT - 1, ps)
                        z_statistics(a, GT - 2)
                    if not project:
                        add_beta(dve, 1, 1)
                    if project:
                        split_k(g, 0)
                        split_k(g, 1)
                        bias_v(g, 0)
                    if attend:
                        z_statistics(a, GT - 1)
                    if project:
                        bias_v(g, 1)
                        split_v(g, 0)
                        if not attend:
                            floor_mu()
                        mask_scores(g)
                    if attend and project:
                        norm_z(dve, a)
                    if project:
                        split_masked(g)
                        split_ktok(g, 0)
                        if more:
                            split_x(g + 1, 0)
                            split_x(g + 1, 1)
                        split_ktok(g, 1)
                    if not project:
                        floor_norms(dve, 0, 0)
                        split_xnT(dve, 0, 0)
                    if attend and project:
                        apply_z(dve, a)

                split_weight(0)
                split_x(0, 0)
                split_x(0, 1)
                for n in range(1, 6):
                    split_weight(n)
                dve.wait_ge(masks_ready, 1)
                dve.wait_ge(rows_loaded, 16 * 3)
                body(0, attend=False, more=False)
                split_x(1, 0)
                split_x(1, 1)
                mu_factors()
                with dve.Fori(1, GROUPS - 1) as g:
                    body(g, attend=True)
                body(GROUPS - 1, attend=True, more=False)
                dve.wait_ge(x1_ready, 2 * GT)
                dve.wait_ge(r2_ready, 2)
                dve.wait_ge(moe_loaded, 16 * 6)
                dve.wait_ge(v_split1, GROUPS)
                body(GROUPS, attend=True, project=False)
                dve.wait_ge(x1_ready, TILES - GT)
                dve.wait_ge(r2_ready, GROUPS - 1)
                dve.wait_ge(shift_ready, 1)
                dve.wait_ge(mu_ready, 1)

        with ExitStack() as moe:
            def msb(name, shape, dt=F32):
                return sb(name, shape, dt, moe)

            def msem(name):
                return sem(name, moe)

            ET_all = msb("ET_all", [P, SB, TILES * P])
            rsum = msb("rsum", [P, TILES])
            rinv = msb("rinv", [P, TILES])
            blank = msb("blank", [P, 12])
            xnT_hi.append(msb("xnT_hi1", [P, KB, GTOK], F32R))
            xnT_lo.append(msb("xnT_lo1", [P, KB, GTOK], F32R))
            e_tok = msb("e_tok", [P, 4, ES])
            colinv = msb("colinv", [P, SB])
            slot_in = msb("slot_in", [P, SB, D])
            slot_inT = msb("slot_inT", [P, KB, B, ES])
            w1_sb = msb("w1_sb", [P, KB, E, H])

            w1_loaded = msem("w1_loaded")
            w2_loaded = msem("w2_loaded")
            ones_set = msem("ones_set")
            logits_done = msem("logits_done")
            e_ready = msem("e_ready")
            eT_done = msem("eT_done")
            eT_ready = msem("eT_ready")
            tile_folded = msem("tile_folded")
            rinv_ready = msem("rinv_ready")
            colinv_ready = msem("colinv_ready")
            slot_in_ready = msem("slot_in_ready")
            slot_in_turned = msem("slot_in_turned")
            slot_inT_ready = msem("slot_inT_ready")

            log_ps, eT_ps, fold_ps = bank[2:4], bank[4:6], bank[6:8]
            slotT_ps = fold_ps[0]
            LEAD = 2

            w2_sb = xn_all[0:H, 0:E * D].rearrange("h (e d) -> h e d", e=E)
            hs = e_tok[0:H, :, :].rearrange("p i (e n) -> p (i e) n", n=B * S)
            soT = slot_inT
            so = w1_sb[:, :, :, :].rearrange("p k (b e) (s h) -> p (k b) (e s h)", b=2, s=1
                                             ).rearrange("p b (s d) -> p b s d", s=SB)
            hs_done = msem("hs_done")
            hs_biased = msem("hs_biased")
            hs_ready = msem("hs_ready")
            soT_done = msem("soT_done")
            soT_ready = msem("soT_ready")
            so_done = msem("so_done")
            so_ready = msem("so_ready")

            eT_flat = slot_inT[:, :, :, :].rearrange("p k b s -> p (k b s)")
            eT = [eT_flat[:, q * SB * GTOK:(q + 1) * SB * GTOK].rearrange("p (s n) -> p s n", s=SB) for q in range(2)]
            y = xn
            st_y = msb("st_y", [P, GT, 6])
            mv_y = msb("mv_y", [P, 2, GT, 2])
            ve_y = msb("ve_y", [P, 2, GT])
            rs_y = msb("rs_y", [P, 2, GT])
            eT_staged = msem("eT_staged")
            mixed = msem("mixed")
            mix_scaled = msem("mix_scaled")
            y_ready = msem("y_ready")
            y_mv = msem("y_mv")
            y_ve = msem("y_ve")
            y_rs = msem("y_rs")
            y_normed = msem("y_normed")
            stored = [msem(f"stored{q}") for q in range(GB)]
            mix_ps = bank[0:4]

            block = moe.enter_context(nc.Block())

            @block.sync
            def _(sp):
                for kb in range(KB):
                    sp.dma_start(w1_sb[:, kb, :, :], w1[:, kb * P:(kb + 1) * P, :].rearrange("e p h -> p e h")
                                 ).then_inc(w1_loaded, 16)
                sp.wait_ge(tile_folded, TILES + TB)
                sp.dma_start(w2_sb[:, :, :], w2.rearrange("e h d -> h e d")).then_inc(w2_loaded, 16)
                with sp.Fori(0, B) as b:
                    for q in range(GB):
                        k = GB * b + q
                        sp.wait_ge(y_normed, GT * k + GT)
                        sp.dma_start(out_t[:, bass.ds(GT * k, GT), :], y[q][:, :, 0:D]).then_inc(stored[q], 16)
                for q in range(GB):
                    sp.wait_ge(stored[q], 16 * B + 16)

            @block.gpsimd
            def _(pool):
                for n, (starts, at) in enumerate(((e_ready, 2), (tile_folded, TB), (eT_ready, 2),
                                                  (slot_inT_ready, 1), (mixed, 2 * GT),
                                                  (mix_scaled, GT), *((stored[q], 16) for q in range(GB)))):
                    pool.memset(blank[:, n:n + 1], 0.0).then_inc(starts, at)
                for q in range(GB):
                    pool.memset(xn[q][:, :, D:D + 1], 1.0).then_inc(ones_set, 1)

                def route(b, last):
                    for q in range(GB):
                        if not (last and q == GB - 1):
                            invert_norms(pool, GB * b + q + 1, (q + 1) % GB, minus_half[:, 0, :])
                        if not (last and q >= GB - 3):
                            add_beta(pool, GB * b + q + 3, (q + 3) % GB)

                add_beta(pool, 2, 2)
                invert_z(pool, GROUPS - 1)
                with pool.Fori(0, B - 1) as b:
                    route(b, last=False)
                route(B - 1, last=True)

                def add_residual(k, q):
                    pool.wait_ge(mix_scaled, GT * k + GT + 4)
                    yq = y[q][:, :, 0:D]
                    pool.tensor_tensor(yq, yq, x1_all[:, bass.ds(GT * k, GT), :], ALU.add).then_inc(y_ready, 1)

                def invert_deviation(k, q):
                    pool.wait_ge(y_ve, k + 1)
                    pool.tensor_tensor(rs_y[:, q % 2, :], ve_y[:, q % 2, :], minus_half[:, 0, :], ALU.pow).then_inc(y_rs, 1)

                def finish(b, last):
                    for q in range(GB):
                        if not (last and q == GB - 1):
                            add_residual(GB * b + q + 1, (q + 1) % GB)
                        invert_deviation(GB * b + q, q)

                add_residual(0, 0)
                with pool.Fori(0, B - 1) as b:
                    finish(b, last=False)
                finish(B - 1, last=True)

            @block.scalar
            def _(act):
                def exps(b, t):
                    q = t // GT % GB
                    act.wait_ge(logits_done, TB * b + t + 1)
                    act.wait_ge(xinv_ready, GB * b + t // GT + 1)
                    nc.scalar.activation(e_tok[:, t % 4, :], log_ps[t % 2][:, 0:ES], ACT.Exp, bias=shift[:, :],
                                         scale=xinv[:, q, t % GT:t % GT + 1],
                                         accum_out=rsum[:, bass.ds(TB * b + t, 1)]).then_inc(e_ready, 1)

                def step(b, t, last):
                    exps(b, t)
                    k, q = GB * b + t // GT + 1, (t // GT + 1) % GB
                    if not (last and q == 0):
                        if t % GT == 0:
                            norms(act, k, q, (0, 1))
                        if t % GT == 1:
                            round_xnT(act, k, q)
                        if t % GT == 2:
                            norms(act, k, q, (2, 3))

                def route(b, last):
                    for t in range(LEAD, TB + (0 if last else LEAD)):
                        step(b, t, last)
                    act.wait_ge(slot_in_turned, b + 1)
                    nc.scalar.copy(slot_inT[:, :, bass.ds(b, 1), :],
                                   slotT_ps[:, :].rearrange("p (k o n) -> p k o n", k=KB, o=1)
                                   ).then_inc(slot_inT_ready, 1)

                for t in range(LEAD):
                    step(0, t, last=False)
                with act.Fori(0, B - 1) as b:
                    route(b, last=False)
                route(B - 1, last=True)
                for half in range(2):
                    act.wait_ge(hs_biased, half + 1)
                    eh = slice(half * E // 2, (half + 1) * E // 2)
                    nc.scalar.activation(hs[:, eh, :], hs[:, eh, :], ACT.Gelu).then_inc(hs_ready, 1)
                for n in range(4):
                    act.wait_ge(so_done, n + 1)
                    nc.scalar.copy(so[:, n, :, :], bank[(6, 7, 0, 1)[n]][:, :].rearrange("p (s d) -> p s d", s=SB)
                                   ).then_inc(so_ready, 1)

                def stage_eT(k, q):
                    act.wait_ge(mixed, GT * k + GT)
                    nc.scalar.copy(eT[q % 2][:, :, :], ET_all[:, :, bass.ds(k * GTOK, GTOK)]
                                   ).then_inc(eT_staged, 1)

                def scale_mix(b, q):
                    k = GB * b + q
                    act.wait_ge(stored[q], 16 * b + 16)
                    for t in range(GT):
                        act.wait_ge(mixed, GT * k + t + 1 + 2 * GT)
                        nc.scalar.activation(y[q][:, t, 0:D], mix_ps[t][:, 0:D], ACT.Copy,
                                             scale=rinv[:, bass.ds(GT * k + t, 1)]).then_inc(mix_scaled, 1)

                def combine(b, last):
                    for q in range(GB):
                        if not (last and q == GB - 1):
                            stage_eT(GB * b + q + 1, (q + 1) % GB)
                        scale_mix(b, q)

                act.wait_ge(eT_ready, TILES + 2)
                act.wait_ge(rinv_ready, B)
                stage_eT(0, 0)
                with act.Fori(0, B - 1) as b:
                    combine(b, last=False)
                combine(B - 1, last=True)

            @block.tensor
            def _(pe):
                def logits(b, t):
                    q = t // GT % GB
                    toks = slice((t % GT) * P, (t % GT + 1) * P)
                    if t % GT == 0:
                        pe.wait_ge(xnT_split, KB * (GB * b + t // GT + 1))
                    pe.wait_ge(e_ready, TB * b + t + 1)
                    ps = log_ps[t % 2][:, 0:ES]
                    for kb in range(KB):
                        hi, lo = xnT_hi[q % 2][:, kb, toks], xnT_lo[q % 2][:, kb, toks]
                        nc.tensor.matmul(ps, hi, mu_hi[:, kb, :], start=(kb == 0), stop=False)
                        nc.tensor.matmul(ps, hi, mu_lo[:, kb, :], start=False, stop=False)
                        last = nc.tensor.matmul(ps, lo, mu_hi[:, kb, :], start=False, stop=(kb == KB - 1))
                    last.then_inc(logits_done, 1)

                def fold(b, t):
                    q = t // GT
                    pe.wait_ge(e_ready, TB * b + t + 3)
                    pe.wait_ge(eT_ready, TB * b + t + 1)
                    for s in range(SB):
                        last = nc.tensor.transpose(eT_ps[t % 2][:, s * P:(s + 1) * P],
                                                   e_tok[:, t % 4, s * P:(s + 1) * P], ident[:, :])
                    last.then_inc(eT_done, 1)
                    if t == 0:
                        pe.wait_ge(slot_inT_ready, b + 1)
                    for s in range(SB):
                        last = nc.tensor.matmul(fold_ps[s][:, 0:D + 1], e_tok[:, t % 4, s * P:(s + 1) * P],
                                                xn[q][:, t % GT, :], start=(t == 0), stop=(t == TB - 1))
                    last.then_inc(tile_folded, 1)

                def lead(b, t, last):
                    logits(b, t)
                    k, q = GB * b + t // GT + 1, (t // GT + 1) % GB
                    if t % GT == 1 and not (last and q == 0):
                        turn_xn(pe, k, q)

                def route(b, last):
                    for t in range(TB):
                        if t < TB - 1 and not (last and t + LEAD >= TB):
                            lead(b, t + LEAD, last)
                        fold(b, t)
                    if not last:
                        lead(b, TB - 1 + LEAD, last)
                    pe.wait_ge(slot_in_ready, SB * b + SB)
                    for db in range(KB):
                        for s in range(SB):
                            at = (db * SB + s) * P
                            done = nc.tensor.transpose(slotT_ps[:, at:at + P],
                                                       slot_in[:, s, db * P:(db + 1) * P], ident[:, :])
                    done.then_inc(slot_in_turned, 1)

                for t in range(LEAD):
                    lead(0, t, last=False)
                pe.wait_ge(ones_set, GB)
                with pe.Fori(0, B - 1) as b:
                    route(b, last=False)
                route(B - 1, last=True)

                pe.wait_ge(w1_loaded, 16 * KB)
                pe.wait_ge(slot_inT_ready, B + 1)
                for e in range(E):
                    ps = bank[2 + e // 8][0:H, (e % 8) * B * S:(e % 8 + 1) * B * S]
                    for kb in range(KB):
                        last = nc.tensor.matmul(ps, w1_sb[:, kb, e, :], slot_inT[:, kb, :, e * S:(e + 1) * S],
                                                start=(kb == 0), stop=(kb == KB - 1))
                    if e % 8 == 7:
                        last.then_inc(hs_done, 1)
                pe.wait_ge(w2_loaded, 16)
                for half in range(2):
                    pe.wait_ge(hs_ready, half + 1)
                    for db in range(KB):
                        ps = bank[(4, 0)[db] + half]
                        for e in range(8 * half, 8 * half + 8):
                            last = nc.tensor.matmul(ps[:, (e % 8) * B * S:(e % 8 + 1) * B * S],
                                                    w2_sb[:, e, db * P:(db + 1) * P], hs[:, e, :],
                                                    start=True, stop=True)
                        last.then_inc(soT_done, 1)
                pe.wait_ge(soT_ready, 4)
                for n in range(B):
                    for s in range(SB):
                        for db in range(KB):
                            at = s * D + db * P
                            last = nc.tensor.transpose(bank[(6, 7, 0, 1)[n]][:, at:at + P],
                                                       soT[:, db, n, s * P:(s + 1) * P], ident[:, :])
                    last.then_inc(so_done, 1)
                pe.wait_ge(so_ready, 4)
                with pe.Fori(0, B) as b:
                    for q in range(GB):
                        k = GB * b + q
                        pe.wait_ge(eT_staged, k + 1)
                        for t in range(GT):
                            pe.wait_ge(mix_scaled, GT * k + t + 1)
                            for s in range(SB):
                                last = nc.tensor.matmul(mix_ps[t][:, 0:D], eT[q % 2][:, s, t * P:(t + 1) * P],
                                                        so[:, bass.ds(b, 1), s, :], start=(s == 0),
                                                        stop=(s == SB - 1))
                            last.then_inc(mixed, 1)

            @block.vector
            def _(dve):
                def copy_eT(b, t):
                    dve.wait_ge(eT_done, TB * b + t + 1)
                    nc.vector.tensor_copy(ET_all[:, :, bass.ds((TB * b + t) * P, P)],
                                          eT_ps[t % 2][:, 0:ES].rearrange("p (s n) -> p s n", s=SB)
                                          ).then_inc(eT_ready, 1)

                def route(b, last):
                    for t in range(TB):
                        q, k = t // GT, GB * b + t // GT
                        copy_eT(b, t)
                        if t == TB - 1:
                            normalise_slots(b)
                        if t % GT == 1 and not (last and q == GB - 1):
                            floor_norms(dve, k + 1, (q + 1) % GB)
                        if t % GT == 2 and not (last and q >= GB - 3):
                            dve.wait_ge(tile_folded, GT * k + 4 * GT)
                            scale_tokens(k + 3, (q + 3) % GB)
                        if t % GT == 3 and not (last and q >= GB - 2):
                            split_xnT(dve, k + 2, (q + 2) % GB)

                def normalise_slots(b):
                    dve.wait_ge(tile_folded, TB * b + 2 * TB)
                    for s in range(SB):
                        nc.vector.reciprocal(colinv[:, s:s + 1], fold_ps[s][:, D:D + 1]).then_inc(colinv_ready, 1)
                    for s in range(SB):
                        dve.wait_ge(colinv_ready, SB * b + s + 1)
                        nc.vector.tensor_scalar(slot_in[:, s, :], fold_ps[s][:, 0:D], colinv[:, s:s + 1], None,
                                                ALU.mult).then_inc(slot_in_ready, 1)
                    nc.vector.reciprocal(rinv[:, bass.ds(TB * b, TB)], rsum[:, bass.ds(TB * b, TB)]
                                         ).then_inc(rinv_ready, 1)

                scale_tokens(2, 2)
                norm_z(dve, GROUPS - 1)
                split_xnT(dve, 1, 1)
                apply_z(dve, GROUPS - 1)
                dve.wait_ge(x1_ready, TILES)
                dve.wait_ge(r2_ready, GROUPS)
                with dve.Fori(0, B - 1) as b:
                    route(b, last=False)
                route(B - 1, last=True)

                for half in range(2):
                    dve.wait_ge(hs_done, half + 1)
                    eh = slice(half * E // 2, (half + 1) * E // 2)
                    nc.vector.tensor_tensor(hs[:, eh, :],
                                            bank[2 + half][0:H, :].rearrange("p (e n) -> p e n", e=E // 2),
                                            b1T[0:H, eh].unsqueeze(2).to_broadcast([H, E // 2, B * S]),
                                            ALU.add).then_inc(hs_biased, 1)
                for half in range(2):
                    for db in range(KB):
                        dve.wait_ge(soT_done, KB * half + db + 1)
                        eh = slice(half * E // 2, (half + 1) * E // 2)
                        for n in range(B):
                            last = nc.vector.tensor_tensor(
                                soT[:, db, n, :].rearrange("p (e s) -> p e s", s=S)[:, eh, :],
                                bank[(4, 0)[db] + half][:, :].rearrange("p (e n s) -> p e n s", n=B, s=S)[:, :, n, :],
                                b2T[:, db, eh].unsqueeze(2).to_broadcast([P, E // 2, S]), ALU.add)
                        last.then_inc(soT_ready, 1)

                def y_statistics(k, q):
                    dve.wait_ge(y_ready, k + 1)
                    for t in range(GT):
                        nc.vector.bn_stats(st_y[:, t, :], y[q][:, t, 0:D])
                    dve.drain()
                    for t in range(GT):
                        nc.vector.bn_aggr(mv_y[:, q % 2, t, :], st_y[:, t, :]).then_inc(y_mv, 1)
                    dve.wait_ge(y_mv, GT * k + GT)
                    nc.vector.tensor_scalar(ve_y[:, q % 2, :], mv_y[:, q % 2, :, 1], LN_EPS, None,
                                            ALU.add).then_inc(y_ve, 1)

                def norm_y(k, q):
                    dve.wait_ge(y_rs, k + 1)
                    for t in range(GT):
                        nc.vector.tensor_scalar(y[q][:, t, 0:D], y[q][:, t, 0:D], mv_y[:, q % 2, t, 0:1],
                                                rs_y[:, q % 2, t:t + 1], ALU.subtract, ALU.mult).then_inc(y_normed, 1)

                def finish(b, last):
                    for q in range(GB):
                        if not (last and q == GB - 1):
                            y_statistics(GB * b + q + 1, (q + 1) % GB)
                        norm_y(GB * b + q, q)

                y_statistics(0, 0)
                with dve.Fori(0, B - 1) as b:
                    finish(b, last=False)
                finish(B - 1, last=True)
        return nc


_INS = ["x", "W1q", "b1q", "W2q", "b2q", "W1k", "b1k", "W2k", "b2k", "W1v", "b1v", "W2v", "b2v", "ln_w", "ln_b",
        "ln_gamma", "ln_beta", "mu", "scale", "w1", "b1", "w2", "b2"]
_NAMES = ["L0_attn_" + n for n in _INS[:15]] + ["L0_ffn_" + n for n in _INS[15:]]


def kernel(**inputs):
    import numpy as _np
    import concourse.bacc as _bacc
    from concourse import mybir as _mybir
    from concourse.bass_utils import run_bass_kernel_spmd as _run

    nc = _bacc.Bacc("TRN2", target_bir_lowering=False, num_devices=1)
    arrays, args = {}, []
    for name in _NAMES:
        a = _np.ascontiguousarray(inputs[name])
        arrays[f"in_{name}"] = a
        args.append(nc.dram_tensor(f"in_{name}", a.shape, _mybir.dt.from_np(a.dtype), kind="ExternalInput").ap())
    shape = inputs["L0_attn_x"].shape
    args.append(nc.dram_tensor("out_0", shape, _mybir.dt.from_np(_np.dtype("float32")), kind="ExternalOutput").ap())
    build(nc, *args)
    r = _run(nc, [arrays], core_ids=[0])
    return r.results[0]["out_0"]
```
